# Optimizing a Trainium2 kernel written in Bass

```python
import numpy as np
import jax
import jax.numpy as jnp

def _softmax(x, axis=-1):
    return jax.nn.softmax(x, axis=axis)

def _gelu(x):
    return jax.nn.gelu(x, approximate=True)

def _silu(x):
    return jax.nn.silu(x)

def _sigmoid(x):
    return jax.nn.sigmoid(x)

def _layernorm(x, axis=-1, eps=1e-05):
    m = jnp.mean(x, axis=axis, keepdims=True)
    v = jnp.var(x, axis=axis, keepdims=True)
    return (x - m) / jnp.sqrt(v + eps)

def _scatter_add(tgt, idx, src, axis=0):
    return tgt.at[idx].add(src)

def _segment_sum(src, seg, n):
    return jax.ops.segment_sum(src, seg, n)
kernel_name = 'mk_seq_postln_d1_jaxref_r8_3e4078'

def setup_inputs(seed: int=0):
    np.random.seed(seed)
    _w = jnp.asarray

    def _L0_attn_setup():
        import jax, jax.numpy as jnp
        import numpy as np
        B, T, D, H = (4, 256, 128, 16)
        HD = D // H
        EPS = 1e-06

        def _phi(x):
            return jax.nn.elu(x) + 1.0

        def _linear_attn(x, Wq, bq, Wk, bk, Wv, bv, Wo, bo):
            b, t, d = x.shape

            def proj(W, bias):
                y = x @ W.T + bias
                return y.reshape(b, t, H, HD).transpose(0, 2, 1, 3)
            qp = _phi(proj(Wq, bq))
            kp = _phi(proj(Wk, bk))
            v = proj(Wv, bv)
            q_tm = qp.transpose(2, 0, 1, 3)
            k_tm = kp.transpose(2, 0, 1, 3)
            v_tm = v.transpose(2, 0, 1, 3)
            kv0 = jnp.zeros((b, H, HD, HD), dtype=x.dtype)
            ks0 = jnp.zeros((b, H, HD), dtype=x.dtype)

            def step(carry, inp):
                kv, ksum = carry
                kt, vt, qt = inp
                kv = kv + jnp.einsum('bhd,bhe->bhde', kt, vt)
                ksum = ksum + kt
                num = jnp.einsum('bhd,bhde->bhe', qt, kv)
                den = jnp.einsum('bhd,bhd->bh', qt, ksum)[..., None] + EPS
                return ((kv, ksum), num / den)
            _, out_tm = jax.lax.scan(step, (kv0, ks0), (k_tm, v_tm, q_tm))
            out = out_tm.transpose(1, 0, 2, 3).reshape(b, t, d)
            return out @ Wo.T + bo
        key = jax.random.key(seed)
        ks = jax.random.split(key, 9)
        s = 1.0 / np.sqrt(D)
        return {'x': jax.random.normal(ks[0], (B, T, D), dtype=jnp.float32), 'Wq': jax.random.normal(ks[1], (D, D), dtype=jnp.float32) * s, 'bq': jnp.zeros((D,), dtype=jnp.float32), 'Wk': jax.random.normal(ks[2], (D, D), dtype=jnp.float32) * s, 'bk': jnp.zeros((D,), dtype=jnp.float32), 'Wv': jax.random.normal(ks[3], (D, D), dtype=jnp.float32) * s, 'bv': jnp.zeros((D,), dtype=jnp.float32), 'Wo': jax.random.normal(ks[4], (D, D), dtype=jnp.float32) * s, 'bo': jnp.zeros((D,), dtype=jnp.float32)}
    _L0_attn_in = _L0_attn_setup()

    def _L0_ffn_setup():
        import jax, jax.numpy as jnp
        import numpy as np
        EMBED = 128
        HEADS = 16
        HEAD_DIM = EMBED // HEADS
        NUM_EXPERTS = 8
        TOP_K = 2
        HIDDEN = (int(2 * (4 * EMBED) / 3) + 63) // 64 * 64
        SEQ = 256
        BATCH = 2
        ROPE_BASE = 10000.0
        EPS = 1e-06

        def _rope_tables(seq_len, dim):
            inv_freq = 1.0 / ROPE_BASE ** (np.arange(0, dim, 2, dtype=np.float32) / dim)
            t = np.arange(seq_len, dtype=np.float32)
            freqs = np.einsum('i,j->ij', t, inv_freq)
            emb = np.concatenate([freqs, freqs], axis=-1)
            return (jnp.asarray(np.cos(emb)), jnp.asarray(np.sin(emb)))

        def _rotate_half(x):
            x1, x2 = jnp.split(x, 2, axis=-1)
            return jnp.concatenate([-x2, x1], axis=-1)

        def _rmsnorm(x, w):
            return x * jax.lax.rsqrt(jnp.mean(x * x, axis=-1, keepdims=True) + EPS) * w

        def _attention(x, wq, wk, wv, wo):
            B, S, _ = x.shape
            q = (x @ wq).reshape(B, S, HEADS, HEAD_DIM).transpose(0, 2, 1, 3)
            k = (x @ wk).reshape(B, S, HEADS, HEAD_DIM).transpose(0, 2, 1, 3)
            v = (x @ wv).reshape(B, S, HEADS, HEAD_DIM).transpose(0, 2, 1, 3)
            cos, sin = _rope_tables(S, HEAD_DIM)
            cos = cos[None, None]
            sin = sin[None, None]
            q = q * cos + _rotate_half(q) * sin
            k = k * cos + _rotate_half(k) * sin
            scale = HEAD_DIM ** (-0.5)
            scores = jnp.einsum('bhqd,bhkd->bhqk', q, k) * scale
            causal = jnp.triu(jnp.ones((S, S), bool), k=1)
            scores = jnp.where(causal, -jnp.inf, scores)
            attn = jax.nn.softmax(scores, axis=-1)
            out = jnp.einsum('bhqk,bhkd->bhqd', attn, v)
            out = out.transpose(0, 2, 1, 3).reshape(B, S, EMBED)
            return out @ wo

        def _moe(x, w_router, wg, wu, wd):
            B, S, E = x.shape
            xf = x.reshape(-1, E)
            logits = xf @ w_router
            probs = jax.nn.softmax(logits, axis=-1)
            topw, topi = jax.lax.top_k(probs, TOP_K)
            topw = topw / jnp.sum(topw, axis=-1, keepdims=True)
            combine = jnp.sum(jax.nn.one_hot(topi, NUM_EXPERTS, dtype=xf.dtype) * topw[..., None], axis=1)
            g = jax.nn.silu(jnp.einsum('td,xdh->txh', xf, wg))
            u = jnp.einsum('td,xdh->txh', xf, wu)
            eo = jnp.einsum('txh,xhd->txd', g * u, wd)
            out = jnp.einsum('txd,tx->td', eo, combine)
            return out.reshape(B, S, E)
        key = jax.random.key(seed)
        ks = jax.random.split(key, 12)
        s = 0.02
        return {'x': jax.random.normal(ks[0], (BATCH, SEQ, EMBED), jnp.float32), 'wq': jax.random.normal(ks[1], (EMBED, EMBED), jnp.float32) * s, 'wk': jax.random.normal(ks[2], (EMBED, EMBED), jnp.float32) * s, 'wv': jax.random.normal(ks[3], (EMBED, EMBED), jnp.float32) * s, 'wo': jax.random.normal(ks[4], (EMBED, EMBED), jnp.float32) * s, 'w_router': jax.random.normal(ks[5], (EMBED, NUM_EXPERTS), jnp.float32) * s, 'wg': jax.random.normal(ks[6], (NUM_EXPERTS, EMBED, HIDDEN), jnp.float32) * s, 'wu': jax.random.normal(ks[7], (NUM_EXPERTS, EMBED, HIDDEN), jnp.float32) * s, 'wd': jax.random.normal(ks[8], (NUM_EXPERTS, HIDDEN, EMBED), jnp.float32) * s, 'g1': jnp.ones((EMBED,), jnp.float32), 'g2': jnp.ones((EMBED,), jnp.float32)}
    _L0_ffn_in = _L0_ffn_setup()
    _d = {'L0_attn_x': _L0_attn_in['x'], 'L0_attn_Wq': _L0_attn_in['Wq'], 'L0_attn_bq': _L0_attn_in['bq'], 'L0_attn_Wk': _L0_attn_in['Wk'], 'L0_attn_bk': _L0_attn_in['bk'], 'L0_attn_Wv': _L0_attn_in['Wv'], 'L0_attn_bv': _L0_attn_in['bv'], 'L0_attn_Wo': _L0_attn_in['Wo'], 'L0_attn_bo': _L0_attn_in['bo'], 'L0_ffn_wq': _L0_ffn_in['wq'], 'L0_ffn_wk': _L0_ffn_in['wk'], 'L0_ffn_wv': _L0_ffn_in['wv'], 'L0_ffn_wo': _L0_ffn_in['wo'], 'L0_ffn_w_router': _L0_ffn_in['w_router'], 'L0_ffn_wg': _L0_ffn_in['wg'], 'L0_ffn_wu': _L0_ffn_in['wu'], 'L0_ffn_wd': _L0_ffn_in['wd'], 'L0_ffn_g1': _L0_ffn_in['g1'], 'L0_ffn_g2': _L0_ffn_in['g2']}
    _x0 = _d['L0_attn_x']
    _d['L0_attn_x'] = jax.random.normal(jax.random.fold_in(jax.random.key(seed), 1), (4, 1024, 128), dtype=_x0.dtype)
    del _x0
    return _d

def reference(L0_attn_x, L0_attn_Wq, L0_attn_bq, L0_attn_Wk, L0_attn_bk, L0_attn_Wv, L0_attn_bv, L0_attn_Wo, L0_attn_bo, L0_ffn_wq, L0_ffn_wk, L0_ffn_wv, L0_ffn_wo, L0_ffn_w_router, L0_ffn_wg, L0_ffn_wu, L0_ffn_wd, L0_ffn_g1, L0_ffn_g2):

    def _L0_attn_ref(x, Wq, bq, Wk, bk, Wv, bv, Wo, bo):
        import jax, jax.numpy as jnp
        import numpy as np
        B, T, D, H = (4, 256, 128, 16)
        HD = D // H
        EPS = 1e-06

        def _phi(x):
            return jax.nn.elu(x) + 1.0

        def _linear_attn(x, Wq, bq, Wk, bk, Wv, bv, Wo, bo):
            b, t, d = x.shape

            def proj(W, bias):
                y = x @ W.T + bias
                return y.reshape(b, t, H, HD).transpose(0, 2, 1, 3)
            qp = _phi(proj(Wq, bq))
            kp = _phi(proj(Wk, bk))
            v = proj(Wv, bv)
            q_tm = qp.transpose(2, 0, 1, 3)
            k_tm = kp.transpose(2, 0, 1, 3)
            v_tm = v.transpose(2, 0, 1, 3)
            kv0 = jnp.zeros((b, H, HD, HD), dtype=x.dtype)
            ks0 = jnp.zeros((b, H, HD), dtype=x.dtype)

            def step(carry, inp):
                kv, ksum = carry
                kt, vt, qt = inp
                kv = kv + jnp.einsum('bhd,bhe->bhde', kt, vt)
                ksum = ksum + kt
                num = jnp.einsum('bhd,bhde->bhe', qt, kv)
                den = jnp.einsum('bhd,bhd->bh', qt, ksum)[..., None] + EPS
                return ((kv, ksum), num / den)
            _, out_tm = jax.lax.scan(step, (kv0, ks0), (k_tm, v_tm, q_tm))
            out = out_tm.transpose(1, 0, 2, 3).reshape(b, t, d)
            return out @ Wo.T + bo
        return _linear_attn(x, Wq, bq, Wk, bk, Wv, bv, Wo, bo)

    def _L0_ffn_ref(x, wq, wk, wv, wo, w_router, wg, wu, wd, g1, g2):
        import jax, jax.numpy as jnp
        import numpy as np
        EMBED = 128
        HEADS = 16
        HEAD_DIM = EMBED // HEADS
        NUM_EXPERTS = 8
        TOP_K = 2
        HIDDEN = (int(2 * (4 * EMBED) / 3) + 63) // 64 * 64
        SEQ = 256
        BATCH = 2
        ROPE_BASE = 10000.0
        EPS = 1e-06

        def _rope_tables(seq_len, dim):
            inv_freq = 1.0 / ROPE_BASE ** (np.arange(0, dim, 2, dtype=np.float32) / dim)
            t = np.arange(seq_len, dtype=np.float32)
            freqs = np.einsum('i,j->ij', t, inv_freq)
            emb = np.concatenate([freqs, freqs], axis=-1)
            return (jnp.asarray(np.cos(emb)), jnp.asarray(np.sin(emb)))

        def _rotate_half(x):
            x1, x2 = jnp.split(x, 2, axis=-1)
            return jnp.concatenate([-x2, x1], axis=-1)

        def _rmsnorm(x, w):
            return x * jax.lax.rsqrt(jnp.mean(x * x, axis=-1, keepdims=True) + EPS) * w

        def _attention(x, wq, wk, wv, wo):
            B, S, _ = x.shape
            q = (x @ wq).reshape(B, S, HEADS, HEAD_DIM).transpose(0, 2, 1, 3)
            k = (x @ wk).reshape(B, S, HEADS, HEAD_DIM).transpose(0, 2, 1, 3)
            v = (x @ wv).reshape(B, S, HEADS, HEAD_DIM).transpose(0, 2, 1, 3)
            cos, sin = _rope_tables(S, HEAD_DIM)
            cos = cos[None, None]
            sin = sin[None, None]
            q = q * cos + _rotate_half(q) * sin
            k = k * cos + _rotate_half(k) * sin
            scale = HEAD_DIM ** (-0.5)
            scores = jnp.einsum('bhqd,bhkd->bhqk', q, k) * scale
            causal = jnp.triu(jnp.ones((S, S), bool), k=1)
            scores = jnp.where(causal, -jnp.inf, scores)
            attn = jax.nn.softmax(scores, axis=-1)
            out = jnp.einsum('bhqk,bhkd->bhqd', attn, v)
            out = out.transpose(0, 2, 1, 3).reshape(B, S, EMBED)
            return out @ wo

        def _moe(x, w_router, wg, wu, wd):
            B, S, E = x.shape
            xf = x.reshape(-1, E)
            logits = xf @ w_router
            probs = jax.nn.softmax(logits, axis=-1)
            topw, topi = jax.lax.top_k(probs, TOP_K)
            topw = topw / jnp.sum(topw, axis=-1, keepdims=True)
            combine = jnp.sum(jax.nn.one_hot(topi, NUM_EXPERTS, dtype=xf.dtype) * topw[..., None], axis=1)
            g = jax.nn.silu(jnp.einsum('td,xdh->txh', xf, wg))
            u = jnp.einsum('td,xdh->txh', xf, wu)
            eo = jnp.einsum('txh,xhd->txd', g * u, wd)
            out = jnp.einsum('txd,tx->td', eo, combine)
            return out.reshape(B, S, E)
        h = x + _attention(_rmsnorm(x, g1), wq, wk, wv, wo)
        y = h + _moe(_rmsnorm(h, g2), w_router, wg, wu, wd)
        return y
    x = L0_attn_x
    x = _layernorm(x + _L0_attn_ref(x, L0_attn_Wq, L0_attn_bq, L0_attn_Wk, L0_attn_bk, L0_attn_Wv, L0_attn_bv, L0_attn_Wo, L0_attn_bo), axis=-1)
    x = _layernorm(x + _L0_ffn_ref(x, L0_ffn_wq, L0_ffn_wk, L0_ffn_wv, L0_ffn_wo, L0_ffn_w_router, L0_ffn_wg, L0_ffn_wu, L0_ffn_wd, L0_ffn_g1, L0_ffn_g2), axis=-1)
    return x

_drawn_inputs = setup_inputs


def setup_inputs(seed=0):
    import zlib

    import numpy as np

    out = dict(_drawn_inputs(seed))
    spreads = {'L0_attn_bq': (0.0, 0.8),
     'L0_attn_bk': (0.0, 0.8),
     'L0_attn_bv': (0.0, 0.1),
     'L0_attn_bo': (0.0, 0.1),
     'L0_ffn_g1': (1.0, 0.6),
     'L0_ffn_g2': (1.0, 0.6)}
    factors = {'L0_attn_Wq': 3.218,
     'L0_ffn_wq': 8.0,
     'L0_ffn_wk': 8.0,
     'L0_ffn_wv': 8.0,
     'L0_ffn_wo': 8.0,
     'L0_ffn_w_router': 8.0,
     'L0_ffn_wg': 8.0,
     'L0_ffn_wu': 8.0,
     'L0_ffn_wd': 8.0}
    for name, (base, spread) in spreads.items():
        noise = np.random.default_rng([zlib.crc32(name.encode()), seed]).standard_normal(out[name].shape)
        drawn = base * np.exp(spread * noise) if base else spread * noise
        out[name] = jnp.asarray(drawn.astype(out[name].dtype))
    for name, factor in factors.items():
        out[name] = (out[name] * factor).astype(out[name].dtype)
    return out
```

```python
from contextlib import ExitStack

import numpy as np
import concourse.bass as bass
from concourse import mybir

F32 = mybir.dt.float32
BF16 = mybir.dt.bfloat16
I32 = mybir.dt.int32
ALU = mybir.AluOpType
ACT = mybir.ActivationFunctionType
AX = mybir.AxisListType

P = 128
B, T, D = 4, 1024, 128
NT = T // P
H, HD = 16, 8
G, J = 4, 4
HALF = 512
E, HID = 8, 384
HT = HID // P
SCALE = float(HD) ** -0.5
LIN_EPS, RMS_EPS, LN_EPS = 1e-6, 1e-6, 1e-5
LOWEST = -3.0e38

Q_RUNS = ((0, 0, 3), (24, 0, 2), (40, 0, 1))
K_RUNS = ((0, 0, 3), (24, 1, 2), (40, 2, 1))
ROWS = 48
STACK_DMAS = 2 * (len(Q_RUNS) + len(K_RUNS)) + 2

W_QL, W_KL, W_VL, W_OL, W_Q, W_QR, W_K, W_KR, W_V, W_O = (i * D for i in range(10))
C_EYE, C_HEAD, C_RANK = 0, P, P + H
C_WIDTH = C_RANK + NT * E

STAGES = 7
LIN_PROJ, LIN_ATTN, LIN_OUT, SOFT_PROJ, SOFT_ATTN, SOFT_OUT, MOE = range(STAGES)


def segments():
    return [(qb, kt, kt == 0, kt == 4 * qb + 3) for qb in range(2) for kt in range(4 * qb + 4)]


STEPS = segments()
NS = len(STEPS)


def score_pieces():
    out = []
    for qt in range(NT):
        if qt >= 4:
            out += [(qt, (j,), 0, HALF, False, 0) for j in range(J)]
        n = (qt % 4 + 1) * P
        per = HALF // n
        out += [(qt, tuple(range(j, min(j + per, J))), (qt // 4) * HALF, n, True, 1) for j in range(0, J, per)]
    return out


PIECES = score_pieces()
NPC = len(PIECES) + 1
SPREAD = 9


def pieces_of(step):
    cut = [min(len(PIECES), -(-len(PIECES) * s // SPREAD)) for s in range(NS + 1)]
    return range(cut[step], cut[step + 1])


def block_program(nc, x_rows, x_cols, attn_w, cols, rows, consts, consts_b, stack_rows, rope, w_router,
                  wg, wu, wd, out):
    with ExitStack() as ctx:
        def sb(name, shape, dt=F32):
            return ctx.enter_context(nc.sbuf_tensor(name, shape, dt))

        def sem(name):
            return ctx.enter_context(nc.semaphore(name))

        W = sb("W", [P, 10 * D])
        WG = sb("WG", [P, E, HID])
        WU = sb("WU", [P, E, HID])
        WD = sb("WD", [P, E * HT, D])
        WR = sb("WR", [P, E])
        COLS = sb("COLS", [P, 4])
        ROWSB = sb("ROWSB", [P, 3 * D])
        CST = sb("CST", [P, C_WIDTH])
        CSTB = sb("CSTB", [P, 2, P], BF16)
        ROPE = sb("ROPE", [P, 2, T])
        XT = sb("XT", [P, T])
        X = sb("X", [P, NT, D])
        QS = sb("QS", [P, H // 2, T], BF16)
        KS = sb("KS", [P, H, T], BF16)
        PARTS = sb("PARTS", [P, 2, 3, HALF], BF16)
        PHI_QT = sb("PHI_QT", [P, T])
        PHI_K = sb("PHI_K", [P, NT, D])
        VL = sb("VL", [P, NT, H, HD + 1])
        VS = sb("VS", [P, NT, H, HD + 1])
        STATE = sb("STATE", [P, NT, H, HD + 1])
        OCOPY = sb("OCOPY", [P, 2, HALF])
        ONORM = sb("ONORM", [P, NT, D])
        X1 = sb("X1", [P, NT, D])
        NRM = sb("NRM", [P, NT, D])
        SUM = sb("SUM", [P, NT, D])
        XNT = sb("XNT", [P, T])
        TMP = sb("TMP", [P, 4, HALF])
        WORK = sb("WORK", [P, 8, HALF])
        OUTB = sb("OUTB", [P, NT, D])
        MXP = sb("MXP", [P, 2, J, NT])
        NMAX = sb("NMAX", [P, J * NT])
        MREM = sb("MREM", [J * NT, P])
        MPARTS = sb("MPARTS", [J * NT, 3, P], BF16)
        SM = sb("SM", [P, 16, NT])
        BN = sb("BN", [P, NT, 6])
        MV = sb("MV", [P, NT, 2])
        LG = sb("LG", [P, 6, NT, E])
        CW = sb("CW", [P, NT, E])
        PS = ctx.enter_context(nc.psum_tensor("PS", [P, 8, HALF], F32))

        q_parts = nc.dram_tensor("q_parts", (H, 3, HD, T), BF16).ap()
        k_parts = nc.dram_tensor("k_parts", (H, 3, HD, T), BF16).ap()
        max_parts = nc.dram_tensor("max_parts", (3, J, T), BF16).ap()

        weights_loaded = sem("weights_loaded")
        moe_weights_loaded = sem("moe_weights_loaded")
        ones_loaded = sem("ones_loaded")
        setup_done = sem("setup_done")
        xt_loaded, x_loaded = sem("xt_loaded"), sem("x_loaded")
        x_used, xt_used = sem("x_used"), sem("xt_used")
        act_stage, dve_stage, pool_stage = sem("act_stage"), sem("dve_stage"), sem("pool_stage")
        proj_full = sem("proj_full")
        phi_terms = sem("phi_terms")
        phi_done = sem("phi_done")
        parts_ready = sem("parts_ready")
        parts_stored = [sem("parts_stored_0"), sem("parts_stored_1")]
        nat_full, nat_added, nat_exp, kv_inputs = sem("nat_full"), sem("nat_added"), sem("nat_exp"), sem("kv_inputs")
        kv_full, state_done = sem("kv_full"), sem("state_done")
        stack_loaded = [sem(f"stack_loaded_{g}") for g in range(G)]
        lin_attn_pe, soft_attn_pe = sem("lin_attn_pe"), sem("soft_attn_pe")
        ls_full, ls_copied, ls_masked, lpv_done = sem("ls_full"), sem("ls_copied"), sem("ls_masked"), sem("lpv_done")
        o_copied, o_turned, o_normed = sem("o_copied"), sem("o_turned"), sem("o_normed")
        ot_full, ot_copied, wo_full = sem("ot_full"), sem("ot_copied"), sem("wo_full")
        residual_done, squares_done, normed = sem("residual_done"), sem("squares_done"), sem("normed")
        nt_full, nt_copied = sem("nt_full"), sem("nt_copied")
        rope_full, rope_read = sem("rope_full"), sem("rope_read")
        v_full = sem("v_full")
        v_copied = sem("v_copied")
        piece_full, piece_done = sem("piece_full"), sem("piece_done")
        negmax_ready, mparts_ready, mparts_stored = sem("negmax_ready"), sem("mparts_ready"), sem("mparts_stored")
        max_loaded = [sem(f"max_loaded_{g}") for g in range(G)]
        st_full, exp_done, p_masked, pv_done = sem("st_full"), sem("exp_done"), sem("p_masked"), sem("pv_done")
        router_full, gap_ready, gap_exp = sem("router_full"), sem("gap_ready"), sem("gap_exp")
        gu_full, silu_done, hid_done, y_full, y_added = (sem("gu_full"), sem("silu_done"), sem("hid_done"),
                                                        sem("y_full"), sem("y_added"))
        out_ready, out_stored = sem("out_ready"), sem("out_stored")
        pool_waits, sp_waits = sem("pool_waits"), sem("sp_waits")

        eye = CST[:, C_EYE:C_EYE + P]
        head_mask = CST[:, C_HEAD:C_HEAD + H].rearrange("p (h o) -> p h o", o=1)
        rank = CST[:, C_RANK:C_RANK + NT * E].rearrange("p (t e) -> p t e", e=E)
        eye_b, bias_b = CSTB[:, 0, :], CSTB[:, 1, :]
        hidden = WORK[:, 0:6, :].rearrange("p (s h) n -> p s h n", s=2)
        probs = WORK[:, :, :].rearrange("p (s j) n -> p s j n", s=2)
        block = ctx.enter_context(nc.Block())

        def gu_bank(n):
            return (0, 2, 5)[n % 3]

        @block.sync
        def _(sp):
            def wait_then(signal, value):
                sp.wait_ge(signal, value)
                sp.sem_inc(sp_waits, 1)

            sp.dma_start(XT[:, :], x_cols[:, 0:T]).then_inc(xt_loaded, 16)
            sp.dma_start(W[:, :], attn_w).then_inc(weights_loaded, 16)
            sp.dma_start(COLS[:, :], cols).then_inc(weights_loaded, 16)
            sp.dma_start(ROWSB[:, :], rows).then_inc(weights_loaded, 16)
            sp.dma_start(CST[:, :], consts).then_inc(weights_loaded, 16)
            sp.dma_start(CSTB[:, :, :], consts_b.rearrange("a p n -> p a n")).then_inc(weights_loaded, 16)
            sp.dma_start(WR[:, :], w_router).then_inc(weights_loaded, 16)
            sp.dma_start(ROPE[:, :, :], rope.rearrange("a p t -> p a t")).then_inc(weights_loaded, 16)
            x_tiles = x_rows.rearrange("(b t p) d -> b p t d", b=B, p=P)
            x_batches = x_cols.rearrange("p (b t) -> b p t", b=B)
            out_tiles = out.rearrange("b (t p) d -> b p t d", p=P)
            sp.dma_start(X[:, :, :], x_tiles[0]).then_inc(x_loaded, 16)
            sp.wait_ge(setup_done, 1)
            sp.dma_start(KS[ROWS:ROWS + 3, 0:H:2, :], stack_rows[1]).then_inc(ones_loaded, 16)
            sp.dma_start(KS[64 + ROWS:64 + ROWS + 3, 1:H:2, :], stack_rows[1]).then_inc(ones_loaded, 16)
            sp.dma_start(WG[:, :, :], wg.rearrange("e d h -> d e h")).then_inc(moe_weights_loaded, 16)
            sp.dma_start(WU[:, :, :], wu.rearrange("e d h -> d e h")).then_inc(moe_weights_loaded, 16)
            sp.dma_start(WD[:, :, :], wd.rearrange("e (t p) d -> p (e t) d", p=P)).then_inc(moe_weights_loaded, 16)

            q_rows = q_parts.rearrange("(g j o) i d t -> g o (i d) j t", g=G, o=2)
            k_rows = k_parts.rearrange("(g j o) i d t -> g o (i d) j t", g=G, o=2)

            def store_parts(b, which):
                for n in range(4):
                    dst = q_parts if n < 2 else k_parts
                    wait_then(parts_ready, (b * 2 + which) * 4 + n + 1)
                    for i in range(3):
                        part = i if n < 2 else 2 - i
                        sp.dma_start(dst[:, part, :, (n % 2) * HALF:(n % 2 + 1) * HALF],
                                     PARTS[:, n % 2, i, :]).then_inc(parts_stored[n % 2], 16)

            def load_stacks(b, which, stack_free):
                for slot in range(2):
                    wait_then(parts_stored[slot], 48 * ((b * 2 + which) * 2 + 3))
                wait_then(stack_free, b + 1)
                for g in range(G):
                    for o in range(2):
                        r = 64 * o
                        for r0, i0, n in Q_RUNS:
                            sp.dma_start(QS[r + r0:r + r0 + n * HD, 2 * g:2 * g + 2, :],
                                         q_rows[g, o, i0 * HD:(i0 + n) * HD]).then_inc(stack_loaded[g], 16)
                        for r0, i0, n in K_RUNS:
                            sp.dma_start(KS[r + r0:r + r0 + n * HD, 4 * g + o:4 * g + o + 3:2, :],
                                         k_rows[g, o, i0 * HD:(i0 + n) * HD]).then_inc(stack_loaded[g], 16)
                        sp.dma_start(QS[r + ROWS:r + ROWS + 3, 2 * g:2 * g + 2, :],
                                     stack_rows[0, :, 0:2, :]).then_inc(stack_loaded[g], 16)

            def load_max(b, g):
                u = b * G + g
                wait_then(mparts_ready, u + 1)
                sp.dma_start(max_parts.rearrange("i j (t q) -> (j t) i q", q=P),
                             MPARTS[:, :, :]).then_inc(mparts_stored, 16)
                wait_then(mparts_stored, 16 * (u + 1))
                src = max_parts.rearrange("i (j o) t -> o i j t", o=2)
                for o in range(2):
                    sp.dma_start(QS[64 * o + ROWS:64 * o + ROWS + 3, 2 * g:2 * g + 2, :],
                                 src[o]).then_inc(max_loaded[g], 16)

            def batch(b, more):
                store_parts(b, 0)
                load_stacks(b, 0, soft_attn_pe)
                store_parts(b, 1)
                load_stacks(b, 1, lin_attn_pe)
                for g in range(G):
                    load_max(b, g)
                if more:
                    wait_then(xt_used, b + 1)
                    sp.dma_start(XT[:, :], x_batches[b + 1]).then_inc(xt_loaded, 16)
                    wait_then(x_used, b + 1)
                    sp.dma_start(X[:, :, :], x_tiles[b + 1]).then_inc(x_loaded, 16)
                wait_then(out_ready, b + 1)
                sp.dma_start(out_tiles[b], OUTB[:, :, :]).then_inc(out_stored, 16)

            with sp.Fori(0, B - 1) as b:
                batch(b, True)
            batch(B - 1, False)
            sp.wait_ge(out_stored, 16 * B + 16)

        @block.tensor
        def _(pe):
            pe.sem_inc(soft_attn_pe, 1)
            pe.wait_ge(weights_loaded, 16 * 7)

            def stage(b, s):
                for done in (act_stage, dve_stage, pool_stage):
                    pe.wait_ge(done, b * STAGES + s + 1)

            def lin_proj(b):
                stage(b, LIN_PROJ)
                pe.wait_ge(xt_loaded, 16 * (b + 1))
                for n in range(4):
                    w = W[:, W_QL:W_QL + D] if n < 2 else W[:, W_KL:W_KL + D]
                    nc.tensor.matmul(PS[:, n, :], w, XT[:, (n % 2) * HALF:(n % 2 + 1) * HALF],
                                     start=True, stop=True).then_inc(proj_full, 1)
                for t in range(NT):
                    last = nc.tensor.matmul(PS[:, 4 + t // 2, (t % 2) * 256:(t % 2) * 256 + 256],
                                            XT[:, t * P:(t + 1) * P], W[:, W_KL:W_KL + 2 * D], start=True, stop=True)
                    if t % 2:
                        last.then_inc(nat_full, 1)
                pe.wait_ge(phi_terms, b * 4 + 4)
                pe.wait_ge(kv_inputs, b + 1)
                pe.sem_inc(xt_used, 1)
                for t in range(NT - 1):
                    last = nc.tensor.matmul(PS[:, t // 3, (t % 3) * 144:(t % 3) * 144 + 144], PHI_K[:, t, :],
                                            VL[:, t, :, :], start=True, stop=True)
                    if t in (2, 5, 6):
                        last.then_inc(kv_full, 1)

            def turn_outputs(b, u, per_batch):
                pe.wait_ge(o_copied, (b * 2 * 8) + u + 1)
                pe.wait_ge(o_normed, (b * 2 * 8) + u + 1)
                for t in range(4):
                    last = nc.tensor.transpose(PS[:, 7, t * P:(t + 1) * P], OCOPY[:, u % 2, t * P:(t + 1) * P], eye)
                last.then_inc(o_turned, 1)

            def lin_attn(b):
                stage(b, LIN_ATTN)
                pe.wait_ge(state_done, b + 1)

                def scores(n):
                    g, c = n // NT, n % NT
                    if c == 0:
                        pe.wait_ge(stack_loaded[g], 16 * STACK_DMAS * (2 * b + 1))
                    if n >= 4:
                        pe.wait_ge(ls_copied, b * 32 + n - 3)
                    for j in range(J):
                        last = nc.tensor.matmul(PS[:, n % 4, j * P:(j + 1) * P],
                                                KS[:, 4 * g + j, c * P:(c + 1) * P],
                                                QS[:, 2 * g + j // 2, c * P:(c + 1) * P], start=True, stop=True)
                    last.then_inc(ls_full, 1)

                def outputs(n):
                    g, c = n // NT, n % NT
                    u = n // 4
                    bank = 4 + u % 2
                    pe.wait_ge(ls_masked, b * 32 + n + 1)
                    if c % 4 == 0 and u >= 2:
                        pe.wait_ge(o_copied, b * 16 + u - 1)
                    cols = slice((c % 4) * P, (c % 4 + 1) * P)
                    for j in range(J):
                        last = nc.tensor.matmul(PS[32 * j:32 * j + HD + 1, bank, cols], VL[:, c, 4 * g + j, :],
                                                WORK[:, n % 4, j * P:(j + 1) * P], start=True, stop=(c == 0),
                                                tile_position=(0, 32 * j))
                    if c:
                        for j in range(J):
                            last = nc.tensor.matmul(PS[32 * j:32 * j + HD + 1, bank, cols],
                                                    STATE[:, c, 4 * g + j, :], PHI_QT[:, c * P:(c + 1) * P],
                                                    start=False, stop=True, tile_position=(0, 32 * j))
                    last.then_inc(lpv_done, 1)

                for n in range(32):
                    scores(n)
                    if n:
                        outputs(n - 1)
                    if n % 4 == 2 and n > 4:
                        turn_outputs(b, n // 4 - 1, 16)
                outputs(31)
                turn_outputs(b, 7, 16)

            def project_out(b, which, w):
                pe.wait_ge(o_normed, b * 16 + 8 * which + 9)
                for t in range(NT):
                    last = nc.tensor.transpose(PS[:, t // 4, (t % 4) * P:(t % 4 + 1) * P], ONORM[:, t, :], eye)
                    if t % 4 == 3:
                        last.then_inc(ot_full, 1)
                for t in range(NT):
                    if t % 4 == 0:
                        pe.wait_ge(ot_copied, (b * 2 + which) * 2 + t // 4 + 1)
                    last = nc.tensor.matmul(PS[:, 2 + t // 4, (t % 4) * P:(t % 4 + 1) * P],
                                            XNT[:, t * P:(t + 1) * P], w, start=True, stop=True)
                    if t % 4 == 3:
                        last.then_inc(wo_full, 1)

            def turn_normed(b, which):
                pe.wait_ge(normed, b * 2 + which + 1)
                for t in range(NT):
                    last = nc.tensor.transpose(PS[:, t // 4, (t % 4) * P:(t % 4 + 1) * P], NRM[:, t, :], eye)
                    if t % 4 == 3:
                        last.then_inc(nt_full, 1)

            def lin_out(b):
                stage(b, LIN_OUT)
                project_out(b, 0, W[:, W_OL:W_OL + D])

            def soft_proj(b):
                stage(b, SOFT_PROJ)
                turn_normed(b, 0)
                pe.wait_ge(nt_copied, (b * 2) * 2 + 2)
                for n in range(4):
                    w, wr = (W_Q, W_QR) if n < 2 else (W_K, W_KR)
                    cols = slice((n % 2) * HALF, (n % 2 + 1) * HALF)
                    nc.tensor.matmul(PS[:, 2 * n, :], W[:, w:w + D], XNT[:, cols], start=True, stop=True)
                    nc.tensor.matmul(PS[:, 2 * n + 1, :], W[:, wr:wr + D], XNT[:, cols],
                                     start=True, stop=True).then_inc(rope_full, 1)
                pe.wait_ge(rope_read, b * 4 + 1)
                for t in range(NT):
                    last = nc.tensor.matmul(PS[:, t // 4, (t % 4) * P:(t % 4 + 1) * P], XNT[:, t * P:(t + 1) * P],
                                            W[:, W_V:W_V + D], start=True, stop=True)
                last.then_inc(v_full, 1)

            def soft_attn(b):
                stage(b, SOFT_ATTN)
                pe.wait_ge(v_copied, b + 1)

                def bank_of_piece(idx):
                    if idx >= 2:
                        pe.wait_ge(piece_done, b * G * NPC + idx - 1)
                    return 5 + idx % 2

                def piece(g, i):
                    qt, heads, k0, n, causal, _ = PIECES[i]
                    if i == 0:
                        pe.wait_ge(stack_loaded[g], 16 * STACK_DMAS * (2 * b + 2))
                    bank = bank_of_piece(g * NPC + i)
                    for m, j in enumerate(heads):
                        last = nc.tensor.matmul(PS[:, bank, m * n:(m + 1) * n],
                                                QS[:, 2 * g + j // 2, qt * P:(qt + 1) * P],
                                                KS[:, 4 * g + j, k0:k0 + n], start=True, stop=not causal)
                        if causal:
                            last = nc.tensor.matmul(PS[:, bank, (m + 1) * n - P:(m + 1) * n], eye_b, bias_b,
                                                    start=False, stop=True)
                    last.then_inc(piece_full, 1)

                def turn_max(g):
                    pe.wait_ge(negmax_ready, b * G + g + 1)
                    bank = bank_of_piece(g * NPC + NPC - 1)
                    nc.tensor.transpose(PS[0:J * NT, bank, 0:P], NMAX[:, :], eye).then_inc(piece_full, 1)

                def scores(g, s, pair):
                    qb, kt, _, _ = STEPS[s]
                    q0 = max(0, kt - 4 * qb) * P
                    n = HALF - q0
                    at = g * NS + s
                    if at >= 1:
                        pe.wait_ge(exp_done, b * 96 + 2 * (at - 1) + pair + 1)
                    for m in range(2):
                        last = nc.tensor.matmul(PS[:, 2 * pair + m, 0:n],
                                                KS[:, 4 * g + 2 * pair + m, kt * P:(kt + 1) * P],
                                                QS[:, 2 * g + pair, qb * HALF + q0:(qb + 1) * HALF],
                                                start=True, stop=True)
                    last.then_inc(st_full, 1)

                def values(g, s):
                    qb, kt, first, final = STEPS[s]
                    q0 = max(0, kt - 4 * qb) * P
                    at = g * NS + s
                    pe.wait_ge(exp_done, b * 96 + 2 * at + 2)
                    if kt >= 4 * qb:
                        pe.wait_ge(p_masked, b * 64 + 2 * (g * 8 + kt) + 2)
                    if first and (g or qb):
                        pe.wait_ge(o_copied, b * 16 + 8 + 2 * g + qb)
                    for j in range(J):
                        last = nc.tensor.matmul(PS[32 * j:32 * j + HD + 1, 4, q0:HALF], VS[:, kt, 4 * g + j, :],
                                                probs[:, at % 2, j, 0:HALF - q0], start=first, stop=final,
                                                tile_position=(0, 32 * j))
                    last.then_inc(pv_done, 1)

                for i in range(len(PIECES)):
                    piece(0, i)
                turn_max(0)
                for g in range(G):
                    pe.wait_ge(max_loaded[g], 32 * (b + 1))
                    for s in range(NS):
                        scores(g, s, 0)
                        todo = list(pieces_of(s)) if g + 1 < G else []
                        for i in todo[:len(todo) // 2]:
                            piece(g + 1, i)
                        scores(g, s, 1)
                        for i in todo[len(todo) // 2:]:
                            piece(g + 1, i)
                        if s or g:
                            values(*divmod(g * NS + s - 1, NS))
                        if s == 1 and g:
                            turn_outputs(b, 8 + 2 * g - 1, 16)
                        if s == 5:
                            turn_outputs(b, 8 + 2 * g, 16)
                        if s == NS - 1 and g + 1 < G:
                            turn_max(g + 1)
                values(G - 1, NS - 1)
                turn_outputs(b, 15, 16)

            def soft_out(b):
                stage(b, SOFT_OUT)
                project_out(b, 1, W[:, W_O:W_O + D])
                turn_normed(b, 1)
                pe.wait_ge(nt_copied, (b * 2 + 1) * 2 + 2)
                for t in range(NT):
                    last = nc.tensor.matmul(PS[:, 2, t * E:(t + 1) * E], XNT[:, t * P:(t + 1) * P], WR[:, :],
                                            start=True, stop=True)
                last.then_inc(router_full, 1)

            def moe(b):
                stage(b, MOE)
                pe.wait_ge(moe_weights_loaded, 48)

                def gate_up(n):
                    tb, e, ht = n // (E * HT), n // HT % E, n % HT
                    if n >= 3:
                        pe.wait_ge(hid_done, b * 48 + n - 2)
                    cols = slice(tb * HALF, (tb + 1) * HALF)
                    bank = gu_bank(n)
                    nc.tensor.matmul(PS[:, bank, :], WG[:, e, ht * P:(ht + 1) * P], XNT[:, cols], start=True, stop=True)
                    nc.tensor.matmul(PS[:, bank + 1, :], WU[:, e, ht * P:(ht + 1) * P], XNT[:, cols],
                                     start=True, stop=True).then_inc(gu_full, 1)

                def down(m):
                    e = m % E
                    pe.wait_ge(hid_done, b * 48 + 3 * m + 3)
                    if m >= 2:
                        pe.wait_ge(y_added, b * 16 + m - 1)
                    for t in range(4):
                        for ht in range(HT):
                            last = nc.tensor.matmul(PS[:, (4, 7)[m % 2], t * P:(t + 1) * P],
                                                    hidden[:, m % 2, ht, t * P:(t + 1) * P], WD[:, e * HT + ht, :],
                                                    start=(ht == 0), stop=(ht == HT - 1))
                    last.then_inc(y_full, 1)

                for n in range(2 * E * HT):
                    gate_up(n)
                    if n % HT == 1 and n > HT:
                        down(n // HT - 1)
                down(2 * E - 1)

            with pe.Fori(0, B) as b:
                lin_proj(b)
                lin_attn(b)
                lin_out(b)
                pe.sem_inc(lin_attn_pe, 1)
                soft_proj(b)
                soft_attn(b)
                soft_out(b)
                pe.sem_inc(soft_attn_pe, 1)
                moe(b)

        @block.scalar
        def _(act):
            act.wait_ge(weights_loaded, 16 * 7)
            act.sem_inc(act_stage, 1)

            def end_stage():
                act.drain().then_inc(act_stage, 1)

            def lin_proj(b):
                for n in range(4):
                    bias = COLS[:, n // 2:n // 2 + 1]
                    act.wait_ge(proj_full, b * 4 + n + 1)
                    if n >= 1:
                        act.wait_ge(phi_done, b * 4 + n)
                    nc.scalar.activation(TMP[:, 0, :], PS[:, n, :], ACT.Exp, bias=bias)
                    nc.scalar.activation(TMP[:, 1, :], PS[:, n, :], ACT.Relu, bias=bias).then_inc(phi_terms, 1)
                act.wait_ge(nat_added, b + 1)
                nc.scalar.activation(OUTB_T(), PHI_K[:, :, :], ACT.Exp).then_inc(nat_exp, 1)
                end_stage()

            def OUTB_T():
                return NRM[:, :, :]

            def lin_attn(b):
                for n in range(32):
                    act.wait_ge(ls_full, b * 32 + n + 1)
                    if n >= 4:
                        act.wait_ge(lpv_done, b * 32 + n - 3)
                    nc.scalar.copy(WORK[:, n % 4, :], PS[:, n % 4, :]).then_inc(ls_copied, 1)
                end_stage()

            def copy_turned(b, which):
                for n in range(2):
                    act.wait_ge(ot_full, (b * 2 + which) * 2 + n + 1)
                    nc.scalar.copy(XNT[:, n * HALF:(n + 1) * HALF], PS[:, n, :]).then_inc(ot_copied, 1)

            def squares(b, which):
                act.wait_ge(residual_done, b * 2 + which + 1)
                src = SUM if which else X1
                nc.scalar.activation(NRM[:, :, :], (TMP_rows if which else src)[:, :, :], ACT.Square).then_inc(squares_done, 1)

            TMP_rows = TMP[:, 0:2, :].rearrange("p a (t d) -> p (a t) d", d=D)

            def gain(b, which):
                for n in range(2):
                    act.wait_ge(nt_full, (b * 2 + which) * 2 + n + 1)
                    nc.scalar.activation(XNT[:, n * HALF:(n + 1) * HALF], PS[:, n, :], ACT.Copy,
                                         scale=COLS[:, 2 + which:3 + which]).then_inc(nt_copied, 1)

            def lin_out(b):
                copy_turned(b, 0)
                squares(b, 0)
                end_stage()

            def soft_proj(b):
                gain(b, 0)
                act.wait_ge(v_full, b + 1)
                for n in range(2):
                    last = nc.scalar.copy(VS[:, 4 * n:4 * n + 4, :, 0:HD],
                                          PS[:, n, :].rearrange("p (t h e) -> p t h e", t=4, h=H))
                last.then_inc(v_copied, 1)
                end_stage()

            def soft_attn(b):
                for at in range(G * NS):
                    qb, kt, _, _ = STEPS[at % NS]
                    n = HALF - max(0, kt - 4 * qb) * P
                    for pair in range(2):
                        act.wait_ge(st_full, b * 96 + 2 * at + pair + 1)
                        if at >= 2 and pair == 0:
                            act.wait_ge(pv_done, b * 48 + at - 1)
                        nc.scalar.activation(probs[:, at % 2, 2 * pair:2 * pair + 2, 0:n],
                                             PS[:, 2 * pair:2 * pair + 2, 0:n], ACT.Exp,
                                             scale=SCALE).then_inc(exp_done, 1)
                end_stage()

            def soft_out(b):
                copy_turned(b, 1)
                squares(b, 1)
                gain(b, 1)
                act.wait_ge(gap_ready, b + 1)
                nc.scalar.activation(SM[:, 5, :], SM[:, 4, :], ACT.Exp).then_inc(gap_exp, 1)
                end_stage()

            def moe(b):
                for n in range(2 * E * HT):
                    act.wait_ge(gu_full, b * 48 + n + 1)
                    if n >= 2:
                        act.wait_ge(hid_done, b * 48 + n - 1)
                    nc.scalar.activation(WORK[:, 6 + n % 2, :], PS[:, gu_bank(n), :], ACT.Silu).then_inc(silu_done, 1)
                end_stage()

            with act.Fori(0, B) as b:
                lin_proj(b)
                lin_attn(b)
                lin_out(b)
                soft_proj(b)
                soft_attn(b)
                soft_out(b)
                moe(b)

        @block.gpsimd
        def _(pool):
            pool.memset(QS[:, :, :], 0.0)
            pool.memset(KS[:, :, :], 0.0)
            pool.drain().then_inc(setup_done, 1)
            pool.sem_inc(pool_stage, 1)
            pool.wait_ge(ones_loaded, 32)

            def wait_then(signal, value):
                pool.wait_ge(signal, value)
                pool.sem_inc(pool_waits, 1)

            def lin_attn(b):
                for n in range(32):
                    wait_then(ls_copied, b * 32 + n + 1)
                    v = WORK[:, n % 4, :].rearrange("p (j q) -> p j q", j=J)
                    pool.affine_select(out=v, in_=v, compare_op=ALU.is_ge, fill=0.0, base=0,
                                       pattern=[[0, J], [1, P]], channel_multiplier=-1).then_inc(ls_masked, 1)

            def soft_attn(b):
                for g in range(G):
                    for s, (qb, kt, _, _) in enumerate(STEPS):
                        if kt < 4 * qb:
                            continue
                        at = g * NS + s
                        for pair in range(2):
                            wait_then(exp_done, b * 96 + 2 * at + pair + 1)
                            v = probs[:, at % 2, 2 * pair:2 * pair + 2, 0:P]
                            pool.affine_select(out=v, in_=v, compare_op=ALU.is_ge, fill=0.0, base=0,
                                               pattern=[[0, 2], [1, P]], channel_multiplier=-1).then_inc(p_masked, 1)

            with pool.Fori(0, B) as b:
                pool.sem_inc(pool_stage, 1)
                lin_attn(b)
                pool.drain().then_inc(pool_stage, 1)
                pool.sem_inc(pool_stage, 2)
                soft_attn(b)
                pool.drain().then_inc(pool_stage, 1)
                pool.sem_inc(pool_stage, 2)

        @block.vector
        def _(dve):
            nc.vector.memset(VL[:, :, :, :], 1.0)
            nc.vector.memset(VS[:, :, :, :], 1.0)
            nc.vector.memset(MXP[:, :, :, :], LOWEST)
            for bank in range(8):
                nc.vector.memset(PS[:, bank, :], 0.0)
            dve.wait_ge(weights_loaded, 16 * 7)
            dve.drain().then_inc(dve_stage, 1)
            dve.sem_inc(o_normed, 1)
            dve.sem_inc(parts_stored[0], 48)
            dve.sem_inc(parts_stored[1], 48)
            dve.sem_inc(out_stored, 16)

            def end_stage():
                dve.drain().then_inc(dve_stage, 1)

            def split(b, which, n, src):
                rem = TMP[:, 2, :]
                dve.wait_ge(parts_stored[n % 2], 48 * ((b * 2 + which) * 2 + n // 2 + 1))
                nc.vector.tensor_copy(PARTS[:, n % 2, 0, :], src)
                dve.drain()
                nc.vector.tensor_tensor(rem, src, PARTS[:, n % 2, 0, :], ALU.subtract)
                dve.drain()
                nc.vector.tensor_copy(PARTS[:, n % 2, 1, :], rem)
                dve.drain()
                nc.vector.tensor_tensor(PARTS[:, n % 2, 2, :], rem, PARTS[:, n % 2, 1, :], ALU.subtract)
                dve.drain().then_inc(parts_ready, 1)

            def rsqrt(y, v, t):
                nc.vector.tensor_scalar(y.bitcast(I32), v.bitcast(I32), -0.5, float(0x5F3759DF), ALU.mult, ALU.add)
                dve.drain()
                for _ in range(4):
                    nc.vector.tensor_tensor(t, y, y, ALU.mult)
                    dve.drain()
                    nc.vector.scalar_tensor_tensor(t, t, -0.5, v, ALU.mult, ALU.mult)
                    dve.drain()
                    nc.vector.scalar_tensor_tensor(y, t, 1.5, y, ALU.add, ALU.mult)
                    dve.drain()

            def lin_proj(b):
                for n in range(4):
                    cols = slice((n % 2) * HALF, (n % 2 + 1) * HALF)
                    phi = PHI_QT[:, cols] if n < 2 else TMP[:, 3, :]
                    dve.wait_ge(phi_terms, b * 4 + n + 1)
                    nc.vector.scalar_tensor_tensor(phi, TMP[:, 0, :], 1.0, TMP[:, 1, :], ALU.min, ALU.add)
                    dve.drain().then_inc(phi_done, 1)
                    split(b, 0, n, phi)
                for t in range(NT):
                    if t % 2 == 0:
                        dve.wait_ge(nat_full, b * 4 + t // 2 + 1)
                    src = PS[:, 4 + t // 2, (t % 2) * 256:(t % 2) * 256 + 256]
                    nc.vector.tensor_tensor(PHI_K[:, t, :], src[:, 0:D], ROWSB[:, 0:D], ALU.add)
                    nc.vector.tensor_tensor(VL[:, t, :, 0:HD], src[:, D:2 * D].rearrange("p (h e) -> p h e", h=H),
                                            ROWSB[:, D:2 * D].rearrange("p (h e) -> p h e", h=H), ALU.add)
                dve.drain().then_inc(nat_added, 1)
                dve.wait_ge(nat_exp, b + 1)
                nc.vector.tensor_scalar(PHI_K[:, :, :], PHI_K[:, :, :], 0.0, None, ALU.max)
                dve.drain()
                nc.vector.scalar_tensor_tensor(PHI_K[:, :, :], NRM[:, :, :], 1.0, PHI_K[:, :, :], ALU.min, ALU.add)
                dve.drain().then_inc(kv_inputs, 1)
                for t in range(NT - 1):
                    if t % 3 == 0:
                        dve.wait_ge(kv_full, b * 3 + t // 3 + 1)
                    src = PS[:, t // 3, (t % 3) * 144:(t % 3) * 144 + 144].rearrange("p (h e) -> p h e", h=H)
                    nc.vector.tensor_tensor(STATE[:, t + 1, :, :], src, head_mask.to_broadcast([P, H, HD + 1]), ALU.mult)
                    if t:
                        dve.drain()
                        nc.vector.tensor_tensor(STATE[:, t + 1, :, :], STATE[:, t + 1, :, :], STATE[:, t, :, :], ALU.add)
                        dve.drain()
                dve.drain().then_inc(state_done, 1)
                end_stage()

            def copy_outputs(u, bank):
                nc.vector.tensor_copy(OCOPY[:, u % 2, :], PS[:, bank, :]).then_inc(o_copied, 1)

            def norm_outputs(b, u, eps):
                g, qb = u % 8 // 2, u % 2
                src = PS[:, 7, :].rearrange("p (t j c) -> p t j c", t=4, j=J)
                den = SM[:, 6:8, :].rearrange("p a b -> p (a b)").rearrange("p (t j o) -> p t j o", t=4, o=1)
                dve.wait_ge(o_turned, b * 16 + u + 1)
                nc.vector.tensor_scalar(den, src[:, :, :, HD:HD + 1], eps, None, ALU.add)
                dve.drain()
                nc.vector.reciprocal(den, den)
                dve.drain()
                for t in range(4):
                    nc.vector.tensor_tensor(
                        ONORM[:, 4 * qb + t, g * 32:g * 32 + 32].rearrange("p (j e) -> p j e", j=J),
                        src[:, t, :, 0:HD], den[:, t, :, :].to_broadcast([P, J, HD]), ALU.mult)
                dve.drain().then_inc(o_normed, 1)

            def lin_attn(b):
                for u in range(8):
                    dve.wait_ge(lpv_done, b * 32 + 4 * u + 4)
                    copy_outputs(u, 4 + u % 2)
                    if u:
                        norm_outputs(b, u - 1, LIN_EPS)
                norm_outputs(b, 7, LIN_EPS)
                end_stage()

            def row_norm(b, which):
                rows = (TMP[:, 0:2, :].rearrange("p a (t d) -> p (a t) d", d=D)) if which else X1[:, :, :]
                dve.wait_ge(squares_done, b * 2 + which + 1)
                nc.vector.tensor_reduce(SM[:, 0, :], NRM[:, :, :], AX.X, ALU.add)
                dve.drain()
                nc.vector.tensor_scalar(SM[:, 1, :], SM[:, 0, :], 1.0 / D, RMS_EPS, ALU.mult, ALU.add)
                dve.drain()
                rsqrt(SM[:, 2, :], SM[:, 1, :], SM[:, 3, :])
                nc.vector.tensor_tensor(NRM[:, :, :], rows,
                                        SM[:, 2, :].rearrange("p (t o) -> p t o", o=1).to_broadcast([P, NT, D]), ALU.mult)
                dve.drain().then_inc(normed, 1)

            def layer_norm(dst, src):
                for t in range(NT):
                    nc.vector.bn_stats(BN[:, t, :], src[:, t, :])
                dve.drain()
                for t in range(NT):
                    nc.vector.bn_aggr(MV[:, t, :], BN[:, t, :])
                dve.drain()
                nc.vector.tensor_scalar(SM[:, 1, :], MV[:, :, 1], LN_EPS, None, ALU.add)
                dve.drain()
                rsqrt(SM[:, 2, :], SM[:, 1, :], SM[:, 3, :])
                for t in range(NT):
                    nc.vector.tensor_scalar(dst[:, t, :], src[:, t, :], MV[:, t, 0:1], SM[:, 2, t:t + 1],
                                            ALU.subtract, ALU.mult)
                dve.drain()

            def four(t, n):
                return t[:, 4 * n:4 * n + 4, :]

            def lin_out(b):
                dve.wait_ge(x_loaded, 16 * (b + 1))
                for n in range(2):
                    dve.wait_ge(wo_full, (b * 2) * 2 + n + 1)
                    nc.vector.tensor_tensor(four(SUM, n), PS[:, 2 + n, :].rearrange("p (t d) -> p t d", d=D),
                                            four(X, n), ALU.add)
                dve.drain().then_inc(x_used, 1)
                nc.vector.tensor_tensor(SUM[:, :, :], SUM[:, :, :],
                                        ROWSB[:, 2 * D:3 * D].rearrange("p (o d) -> p o d", o=1).to_broadcast([P, NT, D]),
                                        ALU.add)
                dve.drain()
                layer_norm(X1, SUM)
                dve.drain().then_inc(residual_done, 1)
                row_norm(b, 0)
                end_stage()

            def soft_proj(b):
                for n in range(4):
                    cols = slice((n % 2) * HALF, (n % 2 + 1) * HALF)
                    dve.wait_ge(rope_full, b * 4 + n + 1)
                    nc.vector.tensor_tensor(TMP[:, 0, :], PS[:, 2 * n, :], ROPE[:, 0, cols], ALU.mult)
                    nc.vector.tensor_tensor(TMP[:, 1, :], PS[:, 2 * n + 1, :], ROPE[:, 1, cols], ALU.mult)
                    dve.drain().then_inc(rope_read, 1)
                    nc.vector.tensor_tensor(TMP[:, 3, :], TMP[:, 0, :], TMP[:, 1, :], ALU.add)
                    dve.drain()
                    split(b, 1, n, TMP[:, 3, :])
                end_stage()

            def soft_attn(b):
                def reduce_piece(g, i):
                    qt, heads, _, n, _, slot = PIECES[i]
                    idx = g * NPC + i
                    dve.wait_ge(piece_full, b * G * NPC + idx + 1)
                    src = PS[:, 5 + idx % 2, 0:n * len(heads)].rearrange("p (m k) -> p m k", k=n)
                    nc.vector.tensor_reduce(MXP[:, slot, heads[0]:heads[0] + len(heads), qt], src,
                                            AX.X, ALU.max).then_inc(piece_done, 1)

                def finish_max(g):
                    dve.drain()
                    nc.vector.tensor_tensor(NMAX[:, :].rearrange("p (j t) -> p j t", j=J), MXP[:, 0, :, :],
                                            MXP[:, 1, :, :], ALU.max)
                    dve.drain()
                    nc.vector.tensor_scalar(NMAX[:, :], NMAX[:, :], -1.0, None, ALU.mult)
                    dve.drain().then_inc(negmax_ready, 1)

                def split_max(g):
                    idx = g * NPC + NPC - 1
                    src = PS[0:J * NT, 5 + idx % 2, 0:P]
                    dve.wait_ge(piece_full, b * G * NPC + idx + 1)
                    nc.vector.tensor_copy(MPARTS[:, 0, :], src)
                    dve.drain()
                    nc.vector.tensor_tensor(MREM[:, :], src, MPARTS[:, 0, :], ALU.subtract)
                    dve.drain().then_inc(piece_done, 1)
                    nc.vector.tensor_copy(MPARTS[:, 1, :], MREM[:, :])
                    dve.drain()
                    nc.vector.tensor_tensor(MPARTS[:, 2, :], MREM[:, :], MPARTS[:, 1, :], ALU.subtract)
                    dve.drain().then_inc(mparts_ready, 1)

                for i in range(len(PIECES)):
                    reduce_piece(0, i)
                finish_max(0)
                split_max(0)
                for g in range(G):
                    for s in range(NS):
                        if g + 1 < G:
                            for i in pieces_of(s):
                                reduce_piece(g + 1, i)
                            if s == SPREAD:
                                finish_max(g + 1)
                        if s == 4 or (s == 0 and g):
                            u = 8 + 2 * g + (0 if s else -1)
                            dve.wait_ge(pv_done, b * 48 + g * NS + s)
                            copy_outputs(u, 4)
                        if s == 5 or (s == 1 and g):
                            norm_outputs(b, 8 + 2 * g + (0 if s == 5 else -1), 0.0)
                    if g + 1 < G:
                        split_max(g + 1)
                dve.wait_ge(pv_done, b * 48 + G * NS)
                copy_outputs(15, 4)
                norm_outputs(b, 15, 0.0)
                end_stage()

            def soft_out(b):
                h = TMP[:, 0:2, :].rearrange("p a (t d) -> p (a t) d", d=D)
                for n in range(2):
                    dve.wait_ge(wo_full, (b * 2 + 1) * 2 + n + 1)
                    nc.vector.tensor_tensor(four(h, n), PS[:, 2 + n, :].rearrange("p (t d) -> p t d", d=D),
                                            four(X1, n), ALU.add)
                dve.drain().then_inc(residual_done, 1)
                nc.vector.tensor_tensor(SUM[:, :, :], h, X1[:, :, :], ALU.add)
                row_norm(b, 1)
                route(b)
                end_stage()

            def route(b):
                lg, eq, one, two = (LG[:, i, :, :] for i in range(4))
                top, second = SM[:, 8, :], SM[:, 9, :]

                def wide(v):
                    return v.rearrange("p (t o) -> p t o", o=1).to_broadcast([P, NT, E])

                def pick(values, best, hot):
                    nc.vector.tensor_reduce(best, values, AX.X, ALU.max)
                    dve.drain()
                    nc.vector.tensor_tensor(eq, values, wide(best), ALU.is_equal)
                    dve.drain()
                    nc.vector.tensor_tensor(eq, eq, rank, ALU.mult)
                    dve.drain()
                    nc.vector.tensor_reduce(SM[:, 10, :], eq, AX.X, ALU.max)
                    dve.drain()
                    nc.vector.tensor_tensor(hot, rank, wide(SM[:, 10, :]), ALU.is_equal)
                    dve.drain()

                dve.wait_ge(router_full, b + 1)
                nc.vector.tensor_copy(lg, PS[:, 2, 0:NT * E].rearrange("p (t e) -> p t e", e=E))
                dve.drain()
                pick(lg, top, one)
                nc.vector.scalar_tensor_tensor(LG[:, 4, :, :], one, LOWEST, lg, ALU.mult, ALU.add)
                dve.drain()
                pick(LG[:, 4, :, :], second, two)
                nc.vector.tensor_tensor(SM[:, 4, :], second, top, ALU.subtract)
                dve.drain().then_inc(gap_ready, 1)
                dve.wait_ge(gap_exp, b + 1)
                nc.vector.tensor_scalar(SM[:, 11, :], SM[:, 5, :], 1.0, None, ALU.add)
                dve.drain()
                nc.vector.reciprocal(SM[:, 12, :], SM[:, 11, :])
                dve.drain()
                nc.vector.tensor_tensor(SM[:, 13, :], SM[:, 12, :], SM[:, 5, :], ALU.mult)
                dve.drain()
                nc.vector.tensor_tensor(one, one, wide(SM[:, 12, :]), ALU.mult)
                nc.vector.tensor_tensor(two, two, wide(SM[:, 13, :]), ALU.mult)
                dve.drain()
                nc.vector.tensor_tensor(CW[:, :, :], one, two, ALU.add)
                dve.drain()

            def moe(b):
                def add_expert(m):
                    tb, e = m // E, m % E
                    dve.wait_ge(y_full, b * 16 + m + 1)
                    for t in range(4):
                        tt = 4 * tb + t
                        last = nc.vector.scalar_tensor_tensor(
                            SUM[:, tt, :], PS[:, (4, 7)[m % 2], t * P:(t + 1) * P], CW[:, tt, e:e + 1], SUM[:, tt, :],
                            ALU.mult, ALU.add)
                    dve.drain().then_inc(y_added, 1)

                for n in range(2 * E * HT):
                    dve.wait_ge(silu_done, b * 48 + n + 1)
                    nc.vector.tensor_tensor(hidden[:, n // HT % 2, n % HT, :], WORK[:, 6 + n % 2, :],
                                            PS[:, gu_bank(n) + 1, :], ALU.mult).then_inc(hid_done, 1)
                    if n % HT == 1 and n > HT:
                        add_expert(n // HT - 1)
                add_expert(2 * E - 1)
                end_stage()
                dve.wait_ge(out_stored, 16 * (b + 1))
                layer_norm(OUTB, SUM)
                dve.drain().then_inc(out_ready, 1)

            with dve.Fori(0, B) as b:
                lin_proj(b)
                lin_attn(b)
                lin_out(b)
                soft_proj(b)
                soft_attn(b)
                soft_out(b)
                moe(b)


def rope_tables():
    inv_freq = 1.0 / 10000.0 ** (np.arange(0, HD, 2, dtype=np.float32) / HD)
    freqs = np.einsum("i,j->ij", np.arange(T, dtype=np.float32), inv_freq)
    emb = np.concatenate([freqs, freqs], axis=-1)
    sign = np.where(np.arange(HD) < HD // 2, -1.0, 1.0).astype(np.float32)
    cos, sin = np.cos(emb), np.sin(emb) * sign
    return np.stack([np.tile(cos.T, (H, 1)), np.tile(sin.T, (H, 1))]).astype(np.float32)


def kernel(**inputs):
    import ml_dtypes
    import concourse.bacc as bacc
    from concourse.bass_utils import run_bass_kernel_spmd

    a = {k: np.asarray(v) for k, v in inputs.items()}
    turn = np.array([h * HD + (d + HD // 2) % HD for h in range(H) for d in range(HD)])
    x = a["L0_attn_x"].reshape(B * T, D)
    bf16 = ml_dtypes.bfloat16
    consts = np.concatenate([
        np.eye(P, dtype=np.float32),
        (np.arange(P)[:, None] // HD == np.arange(H)[None, :]).astype(np.float32),
        np.tile(np.arange(E, 0, -1, dtype=np.float32), (P, NT)),
    ], axis=1)
    causal = np.where(np.arange(P)[None, :] <= np.arange(P)[:, None], 0.0, -1e30)
    arrays = {
        "x_rows": x,
        "x_cols": x.T,
        "attn_w": np.concatenate([
            a["L0_attn_Wq"].T, a["L0_attn_Wk"].T, a["L0_attn_Wv"].T, a["L0_attn_Wo"].T,
            a["L0_ffn_wq"], a["L0_ffn_wq"][:, turn], a["L0_ffn_wk"], a["L0_ffn_wk"][:, turn],
            a["L0_ffn_wv"], a["L0_ffn_wo"]], axis=1),
        "cols": np.stack([a["L0_attn_bq"], a["L0_attn_bk"], a["L0_ffn_g1"], a["L0_ffn_g2"]], axis=1),
        "rows": np.tile(np.concatenate([a["L0_attn_bk"], a["L0_attn_bv"], a["L0_attn_bo"]]), (P, 1)),
        "consts": consts,
        "consts_b": np.stack([np.eye(P), causal]).astype(bf16),
        "stack_rows": np.stack([np.zeros((3, H // 2, T)), np.ones((3, H // 2, T))]).astype(bf16),
        "rope": rope_tables(),
        "w_router": a["L0_ffn_w_router"],
        "wg": a["L0_ffn_wg"],
        "wu": a["L0_ffn_wu"],
        "wd": a["L0_ffn_wd"],
    }
    arrays = {k: np.ascontiguousarray(v) for k, v in arrays.items()}
    nc = bacc.Bacc("TRN2", target_bir_lowering=False, num_devices=1)
    args = [nc.dram_tensor(f"in_{k}", v.shape, mybir.dt.from_np(v.dtype), kind="ExternalInput").ap()
            for k, v in arrays.items()]
    out = nc.dram_tensor("out", (B, T, D), F32, kind="ExternalOutput").ap()
    block_program(nc, *args, out)
    r = run_bass_kernel_spmd(nc, [{f"in_{k}": v for k, v in arrays.items()}], core_ids=[0])
    return r.results[0]["out"]
```

```python
from contextlib import ExitStack

import numpy as np
import concourse.bass as bass
from concourse import mybir

F32 = mybir.dt.float32
BF16 = mybir.dt.bfloat16
I32 = mybir.dt.int32
ALU = mybir.AluOpType
ACT = mybir.ActivationFunctionType
AX = mybir.AxisListType

P = 128
B, T, D = 4, 1024, 128
NT = T // P
H, HD = 16, 8
G, J = 4, 4
HALF = 512
E, HID = 8, 384
HT = HID // P
SCALE = float(HD) ** -0.5
LIN_EPS, RMS_EPS, LN_EPS = 1e-6, 1e-6, 1e-5
LOWEST = -3.0e38

Q_RUNS = ((0, 0, 3), (24, 0, 2), (40, 0, 1))
K_RUNS = ((0, 0, 3), (24, 1, 2), (40, 2, 1))
ROWS = 48
STACK_DMAS = 2 * (len(Q_RUNS) + len(K_RUNS)) + 2

W_QL, W_KL, W_VL, W_OL, W_Q, W_QR, W_K, W_KR, W_V, W_O = (i * D for i in range(10))
C_EYE, C_HEAD, C_RANK = 0, P, P + H
C_WIDTH = C_RANK + NT * E

STEPS = [(qb, kt, kt == 0, kt == 4 * qb + 3) for qb in range(2) for kt in range(4 * qb + 4)]
"""Steps of the softmax attention of a group of heads: (query half, key tile, first, last)."""
NS = len(STEPS)
ATT = G * NS
UNITS = 2 * E * HT
CHUNKS = G * NT


def score_pieces():
    out = []
    for qt in range(NT):
        if qt >= 4:
            out += [(qt, (j,), 0, HALF, False, 0) for j in range(J)]
        n = (qt % 4 + 1) * P
        per = HALF // n
        out += [(qt, tuple(range(j, min(j + per, J))), (qt // 4) * HALF, n, True, 1) for j in range(0, J, per)]
    return out


PIECES = score_pieces()
NPC = len(PIECES) + 1

L_TURN, L_OT, L_WO, L_SUM, L_SQ, L_RMS, L_RSB, L_NRM, L_NT, L_ROUTER = 1, 3, 5, 6, 8, 9, 10, 11, 13, 16
L_ROUTE, L_ROUTE2, L_GAP, L_WEIGHTS = 17, 20, 23, 25
E_TURN, E_OT, E_WO, E_BIAS, E_STATS, E_AGG, E_RSA, E_RSB, E_MS, E_MSB, E_X1, E_NRM, E_NT = range(13)
E_ROPE, E_V, E_MAX = 13, 18, 25
A_JOBS = (32, 33, 34, 35, 36, 37, 38, 39, 44, 45, 46)
A_EXP, A_MAX0, A_PHI = 40, 41, 42
MAX_IN_EXPERTS = 57
MAX_ATT_STEPS = 29


def max_plan():
    where = [("experts", n, MAX_IN_EXPERTS * (n - E_MAX + 1) / (UNITS - E_MAX)) for n in range(E_MAX, UNITS)]
    rest = G * len(PIECES) - MAX_IN_EXPERTS
    where += [("attend", n, MAX_IN_EXPERTS + rest * (n + 1) / MAX_ATT_STEPS) for n in range(A_JOBS[0])]
    plan, done, turn = {}, 0, None
    for phase, n, target in where:
        pieces, finished = [], None
        while done < min(target, G * len(PIECES)) and finished is None:
            g, i = divmod(done, len(PIECES))
            pieces.append((g, i))
            done += 1
            if i == len(PIECES) - 1:
                finished = g
        plan[phase, n] = (turn, pieces, finished)
        turn = finished
        if finished:
            assert phase == "attend" and n + 3 < finished * NS
    assert done == G * len(PIECES) and turn is None
    return plan


PLAN = max_plan()
NOTHING = (None, [], None)


def block_program(nc, x_rows, x_cols, attn_w, cols, rows, consts, consts_b, stack_rows, rope, w_router,
                  wg, wu, wd, out):
    with ExitStack() as ctx:
        def sb(name, shape, dt=F32):
            return ctx.enter_context(nc.sbuf_tensor(name, shape, dt))

        def sem(name):
            return ctx.enter_context(nc.semaphore(name))

        W = sb("W", [P, 10 * D])
        WG = sb("WG", [P, E, HID])
        WU = sb("WU", [P, E, HID])
        WD = sb("WD", [P, E * HT, D])
        WR = sb("WR", [P, E])
        COLS = sb("COLS", [P, 4])
        ROWSB = sb("ROWSB", [P, 3 * D])
        CST = sb("CST", [P, C_WIDTH])
        CSTB = sb("CSTB", [P, 2, P], BF16)
        ROPE = sb("ROPE", [P, 2, T])
        XT = sb("XT", [P, T])
        X = sb("X", [P, NT, D])
        QS = sb("QS", [P, H // 2, T], BF16)
        KS = sb("KS", [P, H, T], BF16)
        PARTS = sb("PARTS", [P, 2, 3, HALF], BF16)
        TERMS = sb("TERMS", [P, 2, HALF])
        SRC = sb("SRC", [P, 2, HALF])
        REM = sb("REM", [P, 2, HALF])
        PHI_QT = sb("PHI_QT", [P, T])
        PHI_K = sb("PHI_K", [P, NT, D])
        VL = sb("VL", [P, NT, H, HD + 1])
        VS = sb("VS", [P, NT, H, HD + 1])
        STATE = sb("STATE", [P, NT, H, HD + 1])
        OCOPY = sb("OCOPY", [P, 2, HALF])
        ONORM = sb("ONORM", [P, NT, D])
        X1 = sb("X1", [P, NT, D])
        HROWS = sb("HROWS", [P, NT, D])
        NRM = sb("NRM", [P, NT, D])
        SUM = sb("SUM", [P, NT, D])
        XNT = sb("XNT", [P, T])
        XAT = sb("XAT", [P, T])
        WORK = sb("WORK", [P, 8, HALF])
        OUTB = sb("OUTB", [P, NT, D])
        MXP = sb("MXP", [P, 2, J, NT])
        NMAX = sb("NMAX", [P, J * NT])
        MREM = sb("MREM", [J * NT, P])
        MPARTS = sb("MPARTS", [J * NT, 3, P], BF16)
        SM = sb("SM", [P, 20, NT])
        BN = sb("BN", [P, NT, 6])
        MV = sb("MV", [P, NT, 2])
        LG = sb("LG", [P, 5, NT, E])
        CW = sb("CW", [P, NT, E])
        PS = ctx.enter_context(nc.psum_tensor("PS", [P, 8, HALF], F32))

        q_parts = nc.dram_tensor("q_parts", (H, 3, HD, T), BF16).ap()
        k_parts = nc.dram_tensor("k_parts", (H, 3, HD, T), BF16).ap()
        max_parts = nc.dram_tensor("max_parts", (3, J, T), BF16).ap()

        weights_loaded = sem("weights_loaded")
        moe_weights_loaded = sem("moe_weights_loaded")
        ones_loaded = sem("ones_loaded")
        setup_done, psum_cleared = sem("setup_done"), sem("psum_cleared")
        xt_loaded, x_loaded = sem("xt_loaded"), sem("x_loaded")
        x_used, xt_used = sem("x_used"), sem("xt_used")
        part1_done, rem_done, part2_done = sem("part1_done"), sem("rem_done"), sem("part2_done")
        parts_ready = sem("parts_ready")
        parts_stored = [sem("parts_stored_0"), sem("parts_stored_1")]
        stack_loaded = [sem(f"stack_loaded_{g}") for g in range(G)]
        proj_full, phi_terms, phi_done = sem("proj_full"), sem("phi_terms"), sem("phi_done")
        nat_full, nat_added, nat_exp, kv_inputs = sem("nat_full"), sem("nat_added"), sem("nat_exp"), sem("kv_inputs")
        kv_full, kv_added, state_done = sem("kv_full"), sem("kv_added"), sem("state_done")
        ls_full, ls_copied, ls_masked, lpv_done = sem("ls_full"), sem("ls_copied"), sem("ls_masked"), sem("lpv_done")
        o_copied, o_turned, o_normed = sem("o_copied"), sem("o_turned"), sem("o_normed")
        lot_full, lot_copied, lwo_full = sem("lot_full"), sem("lot_copied"), sem("lwo_full")
        lnormed, lnt_full, lnt_copied = sem("lnormed"), sem("lnt_full"), sem("lnt_copied")
        sot_full, sot_copied, swo_full = sem("sot_full"), sem("sot_copied"), sem("swo_full")
        h_done, squares_done = sem("h_done"), sem("squares_done")
        snormed, snt_full, snt_copied = sem("snormed"), sem("snt_full"), sem("snt_copied")
        rope_full, rope_read, rope_added = sem("rope_full"), sem("rope_read"), sem("rope_added")
        v_full, v_copied = sem("v_full"), sem("v_copied")
        piece_full, piece_done = sem("piece_full"), sem("piece_done")
        negmax_ready, mparts_ready, mparts_stored = sem("negmax_ready"), sem("mparts_ready"), sem("mparts_stored")
        max_loaded = [sem(f"max_loaded_{g}") for g in range(G)]
        st_full, exp_done, p_masked, pv_done = sem("st_full"), sem("exp_done"), sem("p_masked"), sem("pv_done")
        router_full, router_read, gap_ready, gap_exp = (sem("router_full"), sem("router_read"), sem("gap_ready"),
                                                       sem("gap_exp"))
        gu_full, silu_done, hid_done, y_full, y_added = (sem("gu_full"), sem("silu_done"), sem("hid_done"),
                                                        sem("y_full"), sem("y_added"))
        out_ready, out_stored = sem("out_ready"), sem("out_stored")
        pool_waits, sp_waits = sem("pool_waits"), sem("sp_waits")

        eye = CST[:, C_EYE:C_EYE + P]
        head_mask = CST[:, C_HEAD:C_HEAD + H].rearrange("p (h o) -> p h o", o=1)
        rank = CST[:, C_RANK:C_RANK + NT * E].rearrange("p (t e) -> p t e", e=E)
        eye_b, bias_b = CSTB[:, 0, :], CSTB[:, 1, :]
        hidden = WORK[:, 0:6, :].rearrange("p (s h) n -> p s h n", s=2)
        probs = WORK[:, :, :].rearrange("p (s j) n -> p s j n", s=2)
        block = ctx.enter_context(nc.Block())

        def half(n):
            return slice((n % 2) * HALF, (n % 2 + 1) * HALF)

        def tile(t):
            return slice(t * P, (t + 1) * P)

        def queries_of(at):
            qb, kt, _, _ = STEPS[at % NS]
            q0 = max(0, kt - 4 * qb) * P
            return q0, HALF - q0

        def finished_half(at):
            if at < 0 or not STEPS[at % NS][3]:
                return None
            return 8 + 2 * (at // NS) + STEPS[at % NS][0]

        def causal_steps(at):
            return sum(STEPS[a % NS][1] >= 4 * STEPS[a % NS][0] for a in range(at + 1))

        @block.sync
        def _(sp):
            def wait_then(signal, value):
                sp.wait_ge(signal, value)
                sp.sem_inc(sp_waits, 1)

            x_tiles = x_rows.rearrange("(b t p) d -> b p t d", b=B, p=P)
            x_batches = x_cols.rearrange("p (b t) -> b p t", b=B)
            out_tiles = out.rearrange("b (t p) d -> b p t d", p=P)
            q_rows = q_parts.rearrange("(g j o) i d t -> g o (i d) j t", g=G, o=2)
            k_rows = k_parts.rearrange("(g j o) i d t -> g o (i d) j t", g=G, o=2)

            def store_parts(b, which):
                for n in range(4):
                    dst = q_parts if n < 2 else k_parts
                    wait_then(parts_ready, (b * 2 + which) * 4 + n + 1)
                    for i in range(3):
                        part = i if n < 2 else 2 - i
                        sp.dma_start(dst[:, part, :, half(n)],
                                     PARTS[:, n % 2, i, :]).then_inc(parts_stored[n % 2], 16)

            def load_stacks(b, which, free):
                for slot in range(2):
                    wait_then(parts_stored[slot], 48 * ((b * 2 + which) * 2 + 3))
                for g in range(G):
                    if free is not None:
                        wait_then(*free(g))
                    for o in range(2):
                        r = 64 * o
                        for r0, i0, n in Q_RUNS:
                            sp.dma_start(QS[r + r0:r + r0 + n * HD, 2 * g:2 * g + 2, :],
                                         q_rows[g, o, i0 * HD:(i0 + n) * HD]).then_inc(stack_loaded[g], 16)
                        for r0, i0, n in K_RUNS:
                            sp.dma_start(KS[r + r0:r + r0 + n * HD, 4 * g + o:4 * g + o + 3:2, :],
                                         k_rows[g, o, i0 * HD:(i0 + n) * HD]).then_inc(stack_loaded[g], 16)
                        sp.dma_start(QS[r + ROWS:r + ROWS + 3, 2 * g:2 * g + 2, :],
                                     stack_rows[0, :, 0:2, :]).then_inc(stack_loaded[g], 16)

            def load_max(b, g):
                u = b * G + g
                wait_then(mparts_ready, u + 1)
                sp.dma_start(max_parts.rearrange("i j (t q) -> (j t) i q", q=P),
                             MPARTS[:, :, :]).then_inc(mparts_stored, 16)
                wait_then(mparts_stored, 16 * (u + 1))
                src = max_parts.rearrange("i (j o) t -> o i j t", o=2)
                for o in range(2):
                    sp.dma_start(QS[64 * o + ROWS:64 * o + ROWS + 3, 2 * g:2 * g + 2, :],
                                 src[o]).then_inc(max_loaded[g], 16)

            def load_xt(b):
                wait_then(xt_used, b)
                sp.dma_start(XT[:, :], x_batches[b]).then_inc(xt_loaded, 16)

            def load_x(b):
                wait_then(x_used, b)
                sp.dma_start(X[:, :, :], x_tiles[b]).then_inc(x_loaded, 16)

            def softmax_inputs(b):
                store_parts(b, 1)
                load_stacks(b, 1, lambda g: (lpv_done, (b + 1) * CHUNKS))
                load_max(b, 0)

            def attend(b):
                for g in range(1, G):
                    load_max(b, g)

            def batch(b, more):
                attend(b)
                store_parts(b + 1, 0)
                load_stacks(b + 1, 0, lambda g: (pv_done, b * ATT + (g + 1) * NS))
                softmax_inputs(b + 1)
                if more:
                    load_xt(b + 2)
                    load_x(b + 2)
                store(b)

            def store(b):
                wait_then(out_ready, b + 1)
                sp.dma_start(out_tiles[b], OUTB[:, :, :]).then_inc(out_stored, 16)

            sp.dma_start(XT[:, :], x_batches[0]).then_inc(xt_loaded, 16)
            sp.dma_start(W[:, :], attn_w).then_inc(weights_loaded, 16)
            sp.dma_start(COLS[:, :], cols).then_inc(weights_loaded, 16)
            sp.dma_start(ROWSB[:, :], rows).then_inc(weights_loaded, 16)
            sp.dma_start(CST[:, :], consts).then_inc(weights_loaded, 16)
            sp.dma_start(CSTB[:, :, :], consts_b.rearrange("a p n -> p a n")).then_inc(weights_loaded, 16)
            sp.dma_start(WR[:, :], w_router).then_inc(weights_loaded, 16)
            sp.dma_start(ROPE[:, :, :], rope.rearrange("a p t -> p a t")).then_inc(weights_loaded, 16)
            sp.dma_start(X[:, :, :], x_tiles[0]).then_inc(x_loaded, 16)
            sp.wait_ge(setup_done, 1)
            sp.dma_start(KS[ROWS:ROWS + 3, 0:H:2, :], stack_rows[1]).then_inc(ones_loaded, 16)
            sp.dma_start(KS[64 + ROWS:64 + ROWS + 3, 1:H:2, :], stack_rows[1]).then_inc(ones_loaded, 16)
            store_parts(0, 0)
            load_stacks(0, 0, None)
            load_xt(1)
            sp.dma_start(WG[:, :, :], wg.rearrange("e d h -> d e h")).then_inc(moe_weights_loaded, 16)
            sp.dma_start(WU[:, :, :], wu.rearrange("e d h -> d e h")).then_inc(moe_weights_loaded, 16)
            sp.dma_start(WD[:, :, :], wd.rearrange("e (t p) d -> p (e t) d", p=P)).then_inc(moe_weights_loaded, 16)
            softmax_inputs(0)
            load_x(1)
            with sp.Fori(0, B - 2) as b:
                batch(b, True)
            batch(B - 2, False)
            attend(B - 1)
            store(B - 1)
            sp.wait_ge(out_stored, 16 * B + 16)

        @block.tensor
        def _(pe):
            def project(b, r, first):
                bank = 5 + r % 2
                if r < 4:
                    if r == 0:
                        pe.wait_ge(xt_loaded, 16 * (b + 1))
                        if not first:
                            pe.wait_ge(piece_done, b * G * NPC)
                    if r >= 2:
                        pe.wait_ge(phi_terms, b * 4 + r - 1)
                    w = W[:, W_QL:W_QL + D] if r < 2 else W[:, W_KL:W_KL + D]
                    nc.tensor.matmul(PS[:, bank, :], w, XT[:, half(r)], start=True, stop=True).then_inc(proj_full, 1)
                elif r < 8:
                    if r < 6:
                        pe.wait_ge(phi_terms, b * 4 + r - 1)
                    else:
                        pe.wait_ge(nat_added, b * 4 + r - 5)
                    for m in range(2):
                        last = nc.tensor.matmul(PS[:, bank, m * 256:m * 256 + 256], XT[:, tile(2 * (r - 4) + m)],
                                                W[:, W_KL:W_KL + 2 * D], start=True, stop=True)
                    last.then_inc(nat_full, 1)
                else:
                    if r == 8:
                        pe.wait_ge(kv_inputs, b + 1)
                        pe.sem_inc(xt_used, 1)
                    if r == 10:
                        pe.wait_ge(kv_added, b * 3 + 1)
                    tiles = range(3 * (r - 8), min(3 * (r - 8) + 3, NT - 1))
                    for m, t in enumerate(tiles):
                        last = nc.tensor.matmul(PS[:, bank, m * 144:m * 144 + 144], PHI_K[:, t, :],
                                                VL[:, t, :, :], start=True, stop=True)
                    last.then_inc(kv_full, 1)

            def linear_scores(b, n):
                g, c = n // NT, n % NT
                if c == 0:
                    pe.wait_ge(stack_loaded[g], 16 * STACK_DMAS * (2 * b + 1))
                if n >= 3:
                    pe.wait_ge(ls_copied, b * CHUNKS + n - 2)
                for j in range(J):
                    last = nc.tensor.matmul(PS[:, n % 3, j * P:(j + 1) * P], KS[:, 4 * g + j, tile(c)],
                                            QS[:, 2 * g + j // 2, tile(c)], start=True, stop=True)
                last.then_inc(ls_full, 1)

            def linear_outputs(b, n, first):
                g, c = n // NT, n % NT
                u = n // 4
                cols = slice((c % 4) * P, (c % 4 + 1) * P)
                pe.wait_ge(ls_masked, b * CHUNKS + n + 1)
                if c % 4 == 0:
                    if u >= 2:
                        pe.wait_ge(o_copied, b * 16 + u - 1)
                    elif u == 0 and not first:
                        pe.wait_ge(o_copied, b * 16)
                for j in range(J):
                    last = nc.tensor.matmul(PS[32 * j:32 * j + HD + 1, 4 + u % 2, cols], VL[:, c, 4 * g + j, :],
                                            WORK[:, n % 4, tile(j)], start=True, stop=(c == 0),
                                            tile_position=(0, 32 * j))
                if c:
                    for j in range(J):
                        last = nc.tensor.matmul(PS[32 * j:32 * j + HD + 1, 4 + u % 2, cols],
                                                STATE[:, c, 4 * g + j, :], PHI_QT[:, tile(c)],
                                                start=False, stop=True, tile_position=(0, 32 * j))
                last.then_inc(lpv_done, 1)

            def turn_outputs(b, u):
                pe.wait_ge(o_copied, b * 16 + u + 1)
                pe.wait_ge(o_normed, b * 16 + u + 1)
                for t in range(4):
                    last = nc.tensor.transpose(PS[:, 7, tile(t)], OCOPY[:, u % 2, tile(t)], eye)
                last.then_inc(o_turned, 1)

            def turn_rows(src, banks, full):
                for t in range(NT):
                    last = nc.tensor.transpose(PS[:, banks[t // 4], tile(t % 4)], src[:, t, :], eye)
                    if t % 4 == 3:
                        last.then_inc(full, 1)

            def rows_times(src, w, banks, full):
                for t in range(NT):
                    last = nc.tensor.matmul(PS[:, banks[t // 4], tile(t % 4)], src[:, tile(t)], w,
                                            start=True, stop=True)
                    if t % 4 == 3:
                        last.then_inc(full, 1)

            def soft_output(b, n):
                if n == L_TURN:
                    turn_outputs(b, 15)
                if n == L_OT:
                    pe.wait_ge(o_normed, b * 16 + 17)
                    turn_rows(ONORM, (3, 6), sot_full)
                if n == L_WO:
                    pe.wait_ge(sot_copied, b * 2 + 2)
                    rows_times(XNT, W[:, W_O:W_O + D], (3, 6), swo_full)
                if n == L_NT:
                    pe.wait_ge(snormed, b + 1)
                    turn_rows(NRM, (3, 6), snt_full)
                if n == L_ROUTER:
                    pe.wait_ge(snt_copied, b * 2 + 2)
                    for t in range(NT):
                        last = nc.tensor.matmul(PS[:, 6, t * E:(t + 1) * E], XNT[:, tile(t)], WR[:, :],
                                                start=True, stop=True)
                    last.then_inc(router_full, 1)

            def max_bank(b, idx):
                if idx >= 2:
                    pe.wait_ge(piece_done, b * G * NPC + idx - 1)
                return 5 + idx % 2

            def max_pieces(b, pieces):
                for g, i in pieces:
                    qt, heads, k0, n, causal, _ = PIECES[i]
                    if i == 0:
                        pe.wait_ge(stack_loaded[g], 16 * STACK_DMAS * (2 * b + 2))
                        if g == 0:
                            pe.wait_ge(v_copied, b + 1)
                    bank = max_bank(b, g * NPC + i)
                    for m, j in enumerate(heads):
                        last = nc.tensor.matmul(PS[:, bank, m * n:(m + 1) * n], QS[:, 2 * g + j // 2, tile(qt)],
                                                KS[:, 4 * g + j, k0:k0 + n], start=True, stop=not causal)
                        if causal:
                            last = nc.tensor.matmul(PS[:, bank, (m + 1) * n - P:(m + 1) * n], eye_b, bias_b,
                                                    start=False, stop=True)
                    last.then_inc(piece_full, 1)

            def turn_max(b, g):
                if g is None:
                    return
                pe.wait_ge(negmax_ready, b * G + g + 1)
                bank = max_bank(b, g * NPC + NPC - 1)
                nc.tensor.transpose(PS[0:J * NT, bank, 0:P], NMAX[:, :], eye).then_inc(piece_full, 1)

            def prepare(b, n, first):
                if n == E_TURN:
                    turn_outputs(b, 7)
                if n == E_OT:
                    pe.wait_ge(o_normed, b * 16 + 9)
                    if not first:
                        pe.wait_ge(router_read, b)
                    turn_rows(ONORM, (5, 6), lot_full)
                if n == E_WO:
                    pe.wait_ge(lot_copied, b * 2 + 2)
                    rows_times(XAT, W[:, W_OL:W_OL + D], (5, 6), lwo_full)
                if n == E_NT:
                    pe.wait_ge(lnormed, b + 1)
                    turn_rows(NRM, (5, 6), lnt_full)
                if E_ROPE <= n < E_ROPE + 4:
                    m = n - E_ROPE
                    if m == 0:
                        pe.wait_ge(lnt_copied, b * 2 + 2)
                    else:
                        pe.wait_ge(rope_read, b * 4 + m)
                    w, wr = (W_Q, W_QR) if m < 2 else (W_K, W_KR)
                    nc.tensor.matmul(PS[:, 5, :], W[:, w:w + D], XAT[:, half(m)], start=True, stop=True)
                    nc.tensor.matmul(PS[:, 6, :], W[:, wr:wr + D], XAT[:, half(m)],
                                     start=True, stop=True).then_inc(rope_full, 1)
                if n == E_V:
                    pe.wait_ge(rope_read, b * 4 + 4)
                    rows_times(XAT, W[:, W_V:W_V + D], (5, 6), v_full)
                turn, pieces, _ = PLAN.get(("experts", n), NOTHING)
                turn_max(b, turn)
                max_pieces(b, pieces)

            def scores(b, at, pair):
                g, (qb, kt, _, _) = at // NS, STEPS[at % NS]
                q0, n = queries_of(at)
                if at:
                    pe.wait_ge(exp_done, b * 2 * ATT + 2 * (at - 1) + pair + 1)
                for m in range(2):
                    last = nc.tensor.matmul(PS[:, 2 * pair + m, 0:n], KS[:, 4 * g + 2 * pair + m, tile(kt)],
                                            QS[:, 2 * g + pair, qb * HALF + q0:(qb + 1) * HALF],
                                            start=True, stop=True)
                last.then_inc(st_full, 1)

            def values(b, at):
                g, (qb, kt, first, final) = at // NS, STEPS[at % NS]
                q0, n = queries_of(at)
                pe.wait_ge(exp_done, b * 2 * ATT + 2 * at + 2)
                if kt >= 4 * qb:
                    pe.wait_ge(p_masked, b * 2 * causal_steps(ATT - 1) + 2 * causal_steps(at))
                if first:
                    if at == 0:
                        pe.wait_ge(y_added, b * 2 * E + 2 * E)
                    else:
                        pe.wait_ge(o_copied, b * 16 + 8 + 2 * g + qb)
                for j in range(J):
                    last = nc.tensor.matmul(PS[32 * j:32 * j + HD + 1, 4, q0:HALF], VS[:, kt, 4 * g + j, :],
                                            probs[:, at % 2, j, 0:n], start=first, stop=final,
                                            tile_position=(0, 32 * j))
                last.then_inc(pv_done, 1)

            def attend(b, beside):
                for at in range(ATT):
                    if at % NS == 0:
                        pe.wait_ge(max_loaded[at // NS], 32 * (b + 1))
                    turn, pieces, _ = PLAN.get(("attend", at), NOTHING)
                    scores(b, at, 0)
                    early = 0 if turn is not None else len(pieces) // 2
                    late = len(pieces) if turn is None else 0
                    max_pieces(b, pieces[:early])
                    scores(b, at, 1)
                    max_pieces(b, pieces[early:late])
                    if at:
                        values(b, at - 1)
                    turn_max(b, turn)
                    max_pieces(b, pieces[late:])
                    if finished_half(at - 2) is not None:
                        turn_outputs(b, finished_half(at - 2))
                    if beside and at in A_JOBS:
                        project(b + 1, A_JOBS.index(at), False)
                values(b, ATT - 1)

            def gate_up(b, n):
                tb, e, ht = n // (E * HT), n // HT % E, n % HT
                if n >= 2:
                    pe.wait_ge(hid_done, b * UNITS + n - 1)
                bank = 2 * (n % 2)
                nc.tensor.matmul(PS[:, bank, :], WG[:, e, tile(ht)], XNT[:, half(tb)], start=True, stop=True)
                nc.tensor.matmul(PS[:, bank + 1, :], WU[:, e, tile(ht)], XNT[:, half(tb)],
                                 start=True, stop=True).then_inc(gu_full, 1)

            def down(b, m):
                pe.wait_ge(hid_done, b * UNITS + 3 * m + 3)
                pe.wait_ge(y_added, b * 2 * E + 2 * E + m)
                for t in range(4):
                    for ht in range(HT):
                        last = nc.tensor.matmul(PS[:, 4, tile(t)], hidden[:, m % 2, ht, tile(t)],
                                                WD[:, (m % E) * HT + ht, :], start=(ht == 0), stop=(ht == HT - 1))
                last.then_inc(y_full, 1)

            def linear(b, soft):
                pe.wait_ge(state_done, b + 1)
                for n in range(CHUNKS):
                    linear_scores(b, n)
                    if n:
                        linear_outputs(b, n - 1, not soft)
                    if n % 4 == 2 and n > 4:
                        turn_outputs(b, n // 4 - 1)
                    if soft:
                        soft_output(b - 1, n)
                linear_outputs(b, CHUNKS - 1, not soft)

            def experts(b, beside):
                for n in range(UNITS):
                    gate_up(b, n)
                    if n % HT == 1 and n > HT:
                        down(b, n // HT - 1)
                    if beside:
                        prepare(b + 1, n, False)
                down(b, 2 * E - 1)

            pe.wait_ge(psum_cleared, 1)
            pe.wait_ge(weights_loaded, 16 * 7)
            for r in range(len(A_JOBS)):
                project(0, r, True)
            linear(0, False)
            for n in range(UNITS):
                prepare(0, n, True)
            pe.wait_ge(moe_weights_loaded, 48)
            with pe.Fori(0, B - 1) as b:
                attend(b, True)
                linear(b + 1, True)
                experts(b, True)
            attend(B - 1, False)
            for n in (L_TURN, L_OT, L_WO, L_NT, L_ROUTER):
                soft_output(B - 1, n)
            experts(B - 1, False)

        @block.scalar
        def _(act):
            def part(b, which, n, second, src):
                job = (b * 2 + which) * 4 + n
                if second:
                    act.wait_ge(rem_done, job + 1)
                    nc.scalar.copy(PARTS[:, n % 2, 1, :], REM[:, n % 2, :]).then_inc(part2_done, 1)
                else:
                    act.wait_ge(parts_stored[n % 2], 48 * ((b * 2 + which) * 2 + n // 2 + 1))
                    nc.scalar.copy(PARTS[:, n % 2, 0, :], src).then_inc(part1_done, 1)

            def split_source(n):
                return PHI_QT[:, half(n)] if n < 2 else SRC[:, n % 2, :]

            def project(b, r):
                if r < 4:
                    bias = COLS[:, r // 2:r // 2 + 1]
                    act.wait_ge(proj_full, b * 4 + r + 1)
                    if r:
                        act.wait_ge(phi_done, b * 4 + r)
                    nc.scalar.activation(TERMS[:, 0, :], PS[:, 5 + r % 2, :], ACT.Exp, bias=bias)
                    nc.scalar.activation(TERMS[:, 1, :], PS[:, 5 + r % 2, :], ACT.Relu, bias=bias).then_inc(phi_terms, 1)
                if 1 <= r < 5:
                    act.wait_ge(phi_done, b * 4 + r)
                    part(b, 0, r - 1, False, split_source(r - 1))
                if 2 <= r < 6:
                    part(b, 0, r - 2, True, None)

            def natural_exp(b):
                act.wait_ge(nat_added, b * 4 + 4)
                nc.scalar.activation(NRM[:, :, :], PHI_K[:, :, :], ACT.Exp).then_inc(nat_exp, 1)

            def copy_outputs(u, bank):
                nc.scalar.copy(OCOPY[:, u % 2, :], PS[:, bank, :]).then_inc(o_copied, 1)

            def copy_turned(b, dst, banks, full, done, scale=None):
                for n in range(2):
                    act.wait_ge(full, b * 2 + n + 1)
                    if scale is None:
                        nc.scalar.copy(dst[:, half(n)], PS[:, banks[n], :]).then_inc(done, 1)
                    else:
                        nc.scalar.activation(dst[:, half(n)], PS[:, banks[n], :], ACT.Copy,
                                             scale=scale).then_inc(done, 1)

            def soft_output(b, n):
                if n == L_OT:
                    copy_turned(b, XNT, (3, 6), sot_full, sot_copied)
                if n == L_SQ:
                    act.wait_ge(h_done, b + 1)
                    nc.scalar.activation(NRM[:, :, :], HROWS[:, :, :], ACT.Square).then_inc(squares_done, 1)
                if n == L_NT:
                    copy_turned(b, XNT, (3, 6), snt_full, snt_copied, COLS[:, 3:4])
                if n == L_GAP:
                    act.wait_ge(gap_ready, b + 1)
                    nc.scalar.activation(SM[:, 5, :], SM[:, 4, :], ACT.Exp).then_inc(gap_exp, 1)

            def linear(b, soft):
                for n in range(CHUNKS):
                    act.wait_ge(ls_full, b * CHUNKS + n + 1)
                    if n >= 4:
                        act.wait_ge(lpv_done, b * CHUNKS + n - 3)
                    nc.scalar.copy(WORK[:, n % 4, :], PS[:, n % 3, :]).then_inc(ls_copied, 1)
                    if n % 4 == 0 and n:
                        act.wait_ge(lpv_done, b * CHUNKS + n)
                        copy_outputs(n // 4 - 1, 4 + (n // 4 - 1) % 2)
                    if soft:
                        soft_output(b - 1, n)
                act.wait_ge(lpv_done, b * CHUNKS + CHUNKS)
                copy_outputs(7, 5)

            def prepare(b, n):
                if n == E_OT:
                    copy_turned(b, XAT, (5, 6), lot_full, lot_copied)
                if n == E_NT:
                    copy_turned(b, XAT, (5, 6), lnt_full, lnt_copied, COLS[:, 2:3])
                if E_ROPE < n <= E_ROPE + 4:
                    m = n - E_ROPE - 1
                    act.wait_ge(rope_added, b * 4 + m + 1)
                    part(b, 1, m, False, SRC[:, m % 2, :])
                if E_ROPE + 1 < n <= E_ROPE + 5:
                    part(b, 1, n - E_ROPE - 2, True, None)
                if n == E_V:
                    act.wait_ge(v_full, b * 2 + 2)
                    for m in range(2):
                        last = nc.scalar.copy(VS[:, 4 * m:4 * m + 4, :, 0:HD],
                                              PS[:, 5 + m, :].rearrange("p (t h e) -> p t h e", t=4, h=H))
                    last.then_inc(v_copied, 1)

            def attend(b, beside):
                for at in range(ATT):
                    _, n = queries_of(at)
                    for pair in range(2):
                        act.wait_ge(st_full, b * 2 * ATT + 2 * at + pair + 1)
                        if at >= 2 and pair == 0:
                            act.wait_ge(pv_done, b * G * NS + at - 1)
                        nc.scalar.activation(probs[:, at % 2, 2 * pair:2 * pair + 2, 0:n],
                                             PS[:, 2 * pair:2 * pair + 2, 0:n], ACT.Exp,
                                             scale=SCALE).then_inc(exp_done, 1)
                    if finished_half(at - 1) is not None:
                        act.wait_ge(pv_done, b * G * NS + at)
                        copy_outputs(finished_half(at - 1), 4)
                    if beside and at in A_JOBS:
                        project(b + 1, A_JOBS.index(at))
                    if beside and at == A_EXP:
                        natural_exp(b + 1)
                act.wait_ge(pv_done, b * G * NS + ATT)
                copy_outputs(15, 4)

            def experts(b, beside):
                for n in range(UNITS):
                    act.wait_ge(gu_full, b * UNITS + n + 1)
                    if n >= 2:
                        act.wait_ge(hid_done, b * UNITS + n - 1)
                    nc.scalar.activation(WORK[:, 6 + n % 2, :], PS[:, 2 * (n % 2), :], ACT.Silu).then_inc(silu_done, 1)
                    if beside:
                        prepare(b + 1, n)

            act.wait_ge(weights_loaded, 16 * 7)
            for r in range(8):
                project(0, r)
            natural_exp(0)
            linear(0, False)
            for n in range(UNITS):
                prepare(0, n)
            with act.Fori(0, B - 1) as b:
                attend(b, True)
                linear(b + 1, True)
                experts(b, True)
            attend(B - 1, False)
            for n in (L_OT, L_SQ, L_NT, L_GAP):
                soft_output(B - 1, n)
            experts(B - 1, False)

        @block.gpsimd
        def _(pool):
            def wait_then(signal, value):
                pool.wait_ge(signal, value)
                pool.sem_inc(pool_waits, 1)

            def rest(b, which, n, second, src):
                job = (b * 2 + which) * 4 + n
                if second:
                    pool.wait_ge(part2_done, job + 1)
                    nc.gpsimd.tensor_tensor(PARTS[:, n % 2, 2, :], REM[:, n % 2, :], PARTS[:, n % 2, 1, :],
                                            ALU.subtract).then_inc(parts_ready, 1)
                else:
                    pool.wait_ge(part1_done, job + 1)
                    nc.gpsimd.tensor_tensor(REM[:, n % 2, :], src, PARTS[:, n % 2, 0, :],
                                            ALU.subtract).then_inc(rem_done, 1)

            def project(b, r):
                if 1 <= r < 5:
                    n = r - 1
                    rest(b, 0, n, False, PHI_QT[:, half(n)] if n < 2 else SRC[:, n % 2, :])
                if 2 <= r < 6:
                    rest(b, 0, r - 2, True, None)

            def causal(v, heads, done):
                pool.affine_select(out=v, in_=v, compare_op=ALU.is_ge, fill=0.0, base=0,
                                   pattern=[[0, heads], [1, P]], channel_multiplier=-1).then_inc(done, 1)

            def linear(b):
                for n in range(CHUNKS):
                    wait_then(ls_copied, b * CHUNKS + n + 1)
                    causal(WORK[:, n % 4, :].rearrange("p (j q) -> p j q", j=J), J, ls_masked)

            def prepare(b):
                for n in range(6):
                    if n < 4:
                        if n >= 2:
                            pool.wait_ge(rem_done, (b * 2 + 1) * 4 + n - 1)
                        pool.wait_ge(rope_read, b * 4 + n + 1)
                        nc.gpsimd.tensor_tensor(SRC[:, n % 2, :], TERMS[:, 0, :], TERMS[:, 1, :],
                                                ALU.add).then_inc(rope_added, 1)
                    if 1 <= n < 5:
                        rest(b, 1, n - 1, False, SRC[:, (n - 1) % 2, :])
                    if n >= 2:
                        rest(b, 1, n - 2, True, None)

            def attend(b, beside):
                for at in range(ATT):
                    qb, kt, _, _ = STEPS[at % NS]
                    if kt >= 4 * qb:
                        for pair in range(2):
                            wait_then(exp_done, b * 2 * ATT + 2 * at + pair + 1)
                            causal(probs[:, at % 2, 2 * pair:2 * pair + 2, 0:P], 2, p_masked)
                    if beside and at in A_JOBS:
                        project(b + 1, A_JOBS.index(at))

            pool.memset(QS[:, :, :], 0.0)
            pool.memset(KS[:, :, :], 0.0)
            pool.drain().then_inc(setup_done, 1)
            pool.wait_ge(ones_loaded, 32)
            for r in range(8):
                project(0, r)
            linear(0)
            prepare(0)
            with pool.Fori(0, B - 1) as b:
                attend(b, True)
                linear(b + 1)
                prepare(b + 1)
            attend(B - 1, False)

        @block.vector
        def _(dve):
            def seed(y, v):
                nc.vector.tensor_scalar(y.bitcast(I32), v.bitcast(I32), -0.5, float(0x5F3759DF), ALU.mult, ALU.add)
                dve.drain()

            def newton(y, v, t):
                nc.vector.tensor_tensor(t, y, y, ALU.mult)
                dve.drain()
                nc.vector.scalar_tensor_tensor(t, t, -0.5, v, ALU.mult, ALU.mult)
                dve.drain()
                nc.vector.scalar_tensor_tensor(y, t, 1.5, y, ALU.add, ALU.mult)
                dve.drain()

            def wide(v, n):
                return v.rearrange("p (t o) -> p t o", o=1).to_broadcast([P, NT, n])

            def four(t, n):
                return t[:, 4 * n:4 * n + 4, :]

            def rows_of(bank):
                return PS[:, bank, :].rearrange("p (t d) -> p t d", d=D)

            def project(b, r):
                bank = 5 + r % 2
                if r < 4:
                    phi = PHI_QT[:, half(r)] if r < 2 else SRC[:, r % 2, :]
                    dve.wait_ge(phi_terms, b * 4 + r + 1)
                    nc.vector.scalar_tensor_tensor(phi, TERMS[:, 0, :], 1.0, TERMS[:, 1, :], ALU.min,
                                                   ALU.add).then_inc(phi_done, 1)
                elif r < 8:
                    dve.wait_ge(nat_full, b * 4 + r - 3)
                    for m in range(2):
                        t = 2 * (r - 4) + m
                        src = PS[:, bank, m * 256:m * 256 + 256]
                        nc.vector.tensor_tensor(PHI_K[:, t, :], src[:, 0:D], ROWSB[:, 0:D], ALU.add)
                        nc.vector.tensor_tensor(VL[:, t, :, 0:HD], src[:, D:2 * D].rearrange("p (h e) -> p h e", h=H),
                                                ROWSB[:, D:2 * D].rearrange("p (h e) -> p h e", h=H), ALU.add)
                    dve.drain().then_inc(nat_added, 1)
                else:
                    dve.wait_ge(kv_full, b * 3 + r - 7)
                    for m, t in enumerate(range(3 * (r - 8), min(3 * (r - 8) + 3, NT - 1))):
                        src = PS[:, bank, m * 144:m * 144 + 144].rearrange("p (h e) -> p h e", h=H)
                        nc.vector.tensor_tensor(STATE[:, t + 1, :, :], src, head_mask.to_broadcast([P, H, HD + 1]),
                                                ALU.mult)
                        dve.drain()
                        if t:
                            nc.vector.tensor_tensor(STATE[:, t + 1, :, :], STATE[:, t + 1, :, :], STATE[:, t, :, :],
                                                    ALU.add)
                            dve.drain()
                    dve.drain().then_inc(kv_added, 1)
                    if r == 10:
                        dve.sem_inc(state_done, 1)

            def natural_relu(b):
                dve.wait_ge(nat_exp, b + 1)
                nc.vector.tensor_scalar(PHI_K[:, :, :], PHI_K[:, :, :], 0.0, None, ALU.max)
                dve.drain()

            def natural_phi():
                nc.vector.scalar_tensor_tensor(PHI_K[:, :, :], NRM[:, :, :], 1.0, PHI_K[:, :, :], ALU.min, ALU.add)
                dve.drain().then_inc(kv_inputs, 1)

            def norm_outputs(b, u, eps):
                g, qb = u % 8 // 2, u % 2
                src = PS[:, 7, :].rearrange("p (t j c) -> p t j c", t=4, j=J)
                den = SM[:, 6:8, :].rearrange("p a b -> p (a b)").rearrange("p (t j o) -> p t j o", t=4, o=1)
                dve.wait_ge(o_turned, b * 16 + u + 1)
                if eps:
                    nc.vector.tensor_scalar(den, src[:, :, :, HD:HD + 1], eps, None, ALU.add)
                    dve.drain()
                    nc.vector.reciprocal(den, den)
                else:
                    nc.vector.reciprocal(den, src[:, :, :, HD:HD + 1])
                dve.drain()
                nc.vector.tensor_tensor(
                    ONORM[:, 4 * qb:4 * qb + 4, g * 32:g * 32 + 32].rearrange("p t (j e) -> p t j e", j=J),
                    src[:, :, :, 0:HD], den.to_broadcast([P, 4, J, HD]), ALU.mult)
                dve.drain().then_inc(o_normed, 1)

            def layer_stats(src):
                for t in range(NT):
                    nc.vector.bn_stats(BN[:, t, :], src[:, t, :])
                dve.drain()

            def layer_variance(var):
                for t in range(NT):
                    nc.vector.bn_aggr(MV[:, t, :], BN[:, t, :])
                dve.drain()
                nc.vector.tensor_scalar(var, MV[:, :, 1], LN_EPS, None, ALU.add)
                dve.drain()

            def layer_apply(dst, src, rstd):
                for t in range(NT):
                    nc.vector.tensor_scalar(dst[:, t, :], src[:, t, :], MV[:, t, 0:1], rstd[:, t:t + 1],
                                            ALU.subtract, ALU.mult)
                dve.drain()

            def prepare(b, n):
                var, rstd, tmp, ms, rms = (SM[:, i, :] for i in range(14, 19))
                if n == E_TURN:
                    norm_outputs(b, 7, LIN_EPS)
                if n == E_WO:
                    dve.wait_ge(x_loaded, 16 * (b + 1))
                    for m in range(2):
                        dve.wait_ge(lwo_full, b * 2 + m + 1)
                        nc.vector.tensor_tensor(four(X1, m), rows_of(5 + m), four(X, m), ALU.add)
                    dve.drain().then_inc(x_used, 1)
                if n == E_BIAS:
                    nc.vector.tensor_tensor(X1[:, :, :], X1[:, :, :],
                                            ROWSB[:, 2 * D:3 * D].rearrange("p (o d) -> p o d", o=1).to_broadcast([P, NT, D]),
                                            ALU.add)
                    dve.drain()
                if n == E_STATS:
                    layer_stats(X1)
                if n == E_AGG:
                    layer_variance(var)
                if n == E_RSA:
                    seed(rstd, var)
                    newton(rstd, var, tmp)
                if n == E_RSB:
                    newton(rstd, var, tmp)
                    newton(rstd, var, tmp)
                if n == E_MS:
                    nc.vector.tensor_tensor(tmp, rstd, rstd, ALU.mult)
                    dve.drain()
                    nc.vector.tensor_tensor(ms, tmp, MV[:, :, 1], ALU.mult)
                    dve.drain()
                    nc.vector.tensor_scalar(ms, ms, RMS_EPS, None, ALU.add)
                    dve.drain()
                    seed(rms, ms)
                    newton(rms, ms, tmp)
                if n == E_MSB:
                    newton(rms, ms, tmp)
                    newton(rms, ms, tmp)
                if n == E_X1:
                    layer_apply(X1, X1, rstd)
                if n == E_NRM:
                    nc.vector.tensor_tensor(NRM[:, :, :], X1[:, :, :], wide(rms, D), ALU.mult).then_inc(lnormed, 1)
                if E_ROPE <= n < E_ROPE + 4:
                    m = n - E_ROPE
                    dve.wait_ge(rope_full, b * 4 + m + 1)
                    if m:
                        dve.wait_ge(rope_added, b * 4 + m)
                    nc.vector.tensor_tensor(TERMS[:, 0, :], PS[:, 5, :], ROPE[:, 0, half(m)], ALU.mult)
                    nc.vector.tensor_tensor(TERMS[:, 1, :], PS[:, 6, :], ROPE[:, 1, half(m)],
                                            ALU.mult).then_inc(rope_read, 1)
                maxima(b, *PLAN.get(("experts", n), NOTHING))

            def maxima(b, turned, pieces, finished):
                if turned is not None:
                    idx = turned * NPC + NPC - 1
                    src = PS[0:J * NT, 5 + idx % 2, 0:P]
                    dve.wait_ge(piece_full, b * G * NPC + idx + 1)
                    nc.vector.tensor_copy(MPARTS[:, 0, :], src)
                    dve.drain()
                    nc.vector.tensor_tensor(MREM[:, :], src, MPARTS[:, 0, :], ALU.subtract)
                    dve.drain().then_inc(piece_done, 1)
                    nc.vector.tensor_copy(MPARTS[:, 1, :], MREM[:, :])
                    dve.drain()
                    nc.vector.tensor_tensor(MPARTS[:, 2, :], MREM[:, :], MPARTS[:, 1, :], ALU.subtract)
                    dve.drain().then_inc(mparts_ready, 1)
                for g, i in pieces:
                    qt, heads, _, n, _, slot = PIECES[i]
                    idx = g * NPC + i
                    dve.wait_ge(piece_full, b * G * NPC + idx + 1)
                    src = PS[:, 5 + idx % 2, 0:n * len(heads)].rearrange("p (m k) -> p m k", k=n)
                    nc.vector.tensor_reduce(MXP[:, slot, heads[0]:heads[0] + len(heads), qt], src,
                                            AX.X, ALU.max).then_inc(piece_done, 1)
                if finished is not None:
                    dve.drain()
                    nc.vector.tensor_tensor(NMAX[:, :].rearrange("p (j t) -> p j t", j=J), MXP[:, 0, :, :],
                                            MXP[:, 1, :, :], ALU.max)
                    dve.drain()
                    nc.vector.tensor_scalar(NMAX[:, :], NMAX[:, :], -1.0, None, ALU.mult)
                    dve.drain().then_inc(negmax_ready, 1)

            def attend(b, beside):
                for at in range(ATT):
                    maxima(b, *PLAN.get(("attend", at), NOTHING))
                    if finished_half(at - 2) is not None:
                        norm_outputs(b, finished_half(at - 2), 0.0)
                    if beside:
                        if at in A_JOBS:
                            project(b + 1, A_JOBS.index(at))
                        if at == A_MAX0:
                            natural_relu(b + 1)
                        if at == A_PHI:
                            natural_phi()

            def soft_output(b, n):
                ms, rms, tmp = SM[:, 0, :], SM[:, 1, :], SM[:, 2, :]
                lg, eq, one, two = (LG[:, i, :, :] for i in range(4))
                top, second = SM[:, 8, :], SM[:, 9, :]

                def pick(values, best, hot):
                    nc.vector.tensor_reduce(best, values, AX.X, ALU.max)
                    dve.drain()
                    nc.vector.tensor_tensor(eq, values, wide(best, E), ALU.is_equal)
                    dve.drain()
                    nc.vector.tensor_tensor(eq, eq, rank, ALU.mult)
                    dve.drain()
                    nc.vector.tensor_reduce(SM[:, 10, :], eq, AX.X, ALU.max)
                    dve.drain()
                    nc.vector.tensor_tensor(hot, rank, wide(SM[:, 10, :], E), ALU.is_equal)
                    dve.drain()

                if n == L_TURN:
                    norm_outputs(b, 15, 0.0)
                if n == L_WO:
                    for m, bank in enumerate((3, 6)):
                        dve.wait_ge(swo_full, b * 2 + m + 1)
                        nc.vector.tensor_tensor(four(HROWS, m), rows_of(bank), four(X1, m), ALU.add)
                    dve.drain().then_inc(h_done, 1)
                if n == L_SUM:
                    nc.vector.tensor_tensor(SUM[:, :, :], HROWS[:, :, :], X1[:, :, :], ALU.add)
                if n == L_RMS:
                    dve.wait_ge(squares_done, b + 1)
                    nc.vector.tensor_reduce(ms, NRM[:, :, :], AX.X, ALU.add)
                    dve.drain()
                    nc.vector.tensor_scalar(ms, ms, 1.0 / D, RMS_EPS, ALU.mult, ALU.add)
                    dve.drain()
                    seed(rms, ms)
                    newton(rms, ms, tmp)
                if n == L_RSB:
                    newton(rms, ms, tmp)
                    newton(rms, ms, tmp)
                if n == L_NRM:
                    nc.vector.tensor_tensor(NRM[:, :, :], HROWS[:, :, :], wide(rms, D), ALU.mult).then_inc(snormed, 1)
                if n == L_ROUTE:
                    dve.wait_ge(router_full, b + 1)
                    nc.vector.tensor_copy(lg, PS[:, 6, 0:NT * E].rearrange("p (t e) -> p t e", e=E))
                    dve.drain().then_inc(router_read, 1)
                    pick(lg, top, one)
                if n == L_ROUTE2:
                    nc.vector.scalar_tensor_tensor(LG[:, 4, :, :], one, LOWEST, lg, ALU.mult, ALU.add)
                    dve.drain()
                    pick(LG[:, 4, :, :], second, two)
                    nc.vector.tensor_tensor(SM[:, 4, :], second, top, ALU.subtract)
                    dve.drain().then_inc(gap_ready, 1)
                if n == L_WEIGHTS:
                    dve.wait_ge(gap_exp, b + 1)
                    nc.vector.tensor_scalar(SM[:, 11, :], SM[:, 5, :], 1.0, None, ALU.add)
                    dve.drain()
                    nc.vector.reciprocal(SM[:, 12, :], SM[:, 11, :])
                    dve.drain()
                    nc.vector.tensor_tensor(SM[:, 13, :], SM[:, 12, :], SM[:, 5, :], ALU.mult)
                    dve.drain()
                    nc.vector.tensor_tensor(one, one, wide(SM[:, 12, :], E), ALU.mult)
                    nc.vector.tensor_tensor(two, two, wide(SM[:, 13, :], E), ALU.mult)
                    dve.drain()
                    nc.vector.tensor_tensor(CW[:, :, :], one, two, ALU.add)
                    dve.drain()

            def linear(b, soft):
                for n in range(CHUNKS):
                    if n % 4 == 2 and n > 4:
                        norm_outputs(b, n // 4 - 1, LIN_EPS)
                    if soft:
                        soft_output(b - 1, n)

            def experts(b, beside):
                def add_expert(m):
                    tb, e = m // E, m % E
                    dve.wait_ge(y_full, b * 2 * E + m + 1)
                    for t in range(4):
                        tt = 4 * tb + t
                        nc.vector.scalar_tensor_tensor(SUM[:, tt, :], PS[:, 4, tile(t)], CW[:, tt, e:e + 1],
                                                       SUM[:, tt, :], ALU.mult, ALU.add)
                    dve.drain().then_inc(y_added, 1)

                for n in range(UNITS):
                    dve.wait_ge(silu_done, b * UNITS + n + 1)
                    nc.vector.tensor_tensor(hidden[:, n // HT % 2, n % HT, :], WORK[:, 6 + n % 2, :],
                                            PS[:, 2 * (n % 2) + 1, :], ALU.mult).then_inc(hid_done, 1)
                    if n % HT == 1 and n > HT:
                        add_expert(n // HT - 1)
                    if beside:
                        prepare(b + 1, n)
                add_expert(2 * E - 1)
                var, rstd, tmp = SM[:, 1, :], SM[:, 2, :], SM[:, 3, :]
                layer_stats(SUM)
                layer_variance(var)
                seed(rstd, var)
                for _ in range(3):
                    newton(rstd, var, tmp)
                dve.wait_ge(out_stored, 16 * (b + 1))
                layer_apply(OUTB, SUM, rstd)
                dve.drain().then_inc(out_ready, 1)

            for bank in range(8):
                nc.vector.memset(PS[:, bank, :], 0.0)
            dve.drain().then_inc(psum_cleared, 1)
            nc.vector.memset(VL[:, :, :, :], 1.0)
            nc.vector.memset(VS[:, :, :, :], 1.0)
            nc.vector.memset(MXP[:, :, :, :], LOWEST)
            dve.drain()
            dve.sem_inc(o_normed, 1)
            dve.sem_inc(parts_stored[0], 48)
            dve.sem_inc(parts_stored[1], 48)
            dve.sem_inc(y_added, 2 * E)
            dve.sem_inc(out_stored, 16)
            dve.wait_ge(weights_loaded, 16 * 7)
            for r in range(8):
                project(0, r)
            natural_relu(0)
            natural_phi()
            for r in range(8, len(A_JOBS)):
                project(0, r)
            linear(0, False)
            for n in range(UNITS):
                prepare(0, n)
            with dve.Fori(0, B - 1) as b:
                attend(b, True)
                linear(b + 1, True)
                experts(b, True)
            attend(B - 1, False)
            for n in (L_TURN, L_WO, L_SUM, L_RMS, L_RSB, L_NRM, L_ROUTE, L_ROUTE2, L_WEIGHTS):
                soft_output(B - 1, n)
            experts(B - 1, False)


def rope_tables():
    inv_freq = 1.0 / 10000.0 ** (np.arange(0, HD, 2, dtype=np.float32) / HD)
    freqs = np.einsum("i,j->ij", np.arange(T, dtype=np.float32), inv_freq)
    emb = np.concatenate([freqs, freqs], axis=-1)
    sign = np.where(np.arange(HD) < HD // 2, -1.0, 1.0).astype(np.float32)
    cos, sin = np.cos(emb), np.sin(emb) * sign
    return np.stack([np.tile(cos.T, (H, 1)), np.tile(sin.T, (H, 1))]).astype(np.float32)


def kernel(**inputs):
    import ml_dtypes
    import concourse.bacc as bacc
    from concourse.bass_utils import run_bass_kernel_spmd

    a = {k: np.asarray(v) for k, v in inputs.items()}
    turn = np.array([h * HD + (d + HD // 2) % HD for h in range(H) for d in range(HD)])
    x = a["L0_attn_x"].reshape(B * T, D)
    bf16 = ml_dtypes.bfloat16
    consts = np.concatenate([
        np.eye(P, dtype=np.float32),
        (np.arange(P)[:, None] // HD == np.arange(H)[None, :]).astype(np.float32),
        np.tile(np.arange(E, 0, -1, dtype=np.float32), (P, NT)),
    ], axis=1)
    causal = np.where(np.arange(P)[None, :] <= np.arange(P)[:, None], 0.0, -1e30)
    arrays = {
        "x_rows": x,
        "x_cols": x.T,
        "attn_w": np.concatenate([
            a["L0_attn_Wq"].T, a["L0_attn_Wk"].T, a["L0_attn_Wv"].T, a["L0_attn_Wo"].T,
            a["L0_ffn_wq"], a["L0_ffn_wq"][:, turn], a["L0_ffn_wk"], a["L0_ffn_wk"][:, turn],
            a["L0_ffn_wv"], a["L0_ffn_wo"]], axis=1),
        "cols": np.stack([a["L0_attn_bq"], a["L0_attn_bk"], a["L0_ffn_g1"], a["L0_ffn_g2"]], axis=1),
        "rows": np.tile(np.concatenate([a["L0_attn_bk"], a["L0_attn_bv"], a["L0_attn_bo"]]), (P, 1)),
        "consts": consts,
        "consts_b": np.stack([np.eye(P), causal]).astype(bf16),
        "stack_rows": np.stack([np.zeros((3, H // 2, T)), np.ones((3, H // 2, T))]).astype(bf16),
        "rope": rope_tables(),
        "w_router": a["L0_ffn_w_router"],
        "wg": a["L0_ffn_wg"],
        "wu": a["L0_ffn_wu"],
        "wd": a["L0_ffn_wd"],
    }
    arrays = {k: np.ascontiguousarray(v) for k, v in arrays.items()}
    nc = bacc.Bacc("TRN2", target_bir_lowering=False, num_devices=1)
    args = [nc.dram_tensor(f"in_{k}", v.shape, mybir.dt.from_np(v.dtype), kind="ExternalInput").ap()
            for k, v in arrays.items()]
    out = nc.dram_tensor("out", (B, T, D), F32, kind="ExternalOutput").ap()
    block_program(nc, *args, out)
    r = run_bass_kernel_spmd(nc, [{f"in_{k}": v for k, v in arrays.items()}], core_ids=[0])
    return r.results[0]["out"]
```

```python
from contextlib import ExitStack

import numpy as np
import concourse.bass as bass
from concourse import mybir

F32 = mybir.dt.float32
F32R = mybir.dt.float32r
BF16 = mybir.dt.bfloat16
I32 = mybir.dt.int32
ALU = mybir.AluOpType
ACT = mybir.ActivationFunctionType
AX = mybir.AxisListType

P = 128
B, T, D = 4, 1024, 128
NT = T // P
H, HD = 16, 8
G, J = 4, 4
HALF = 512
E, HID = 8, 384
HT = HID // P
SCALE = float(HD) ** -0.5
LIN_EPS, RMS_EPS, LN_EPS = 1e-6, 1e-6, 1e-5
LOWEST = -3.0e38

Q_RUNS = ((0, 0, 3), (24, 0, 2), (40, 0, 1))
K_RUNS = ((0, 0, 3), (24, 1, 2), (40, 2, 1))
ROWS = 48
LINEAR_DMAS = 2 * (len(Q_RUNS) + len(K_RUNS)) + 2
STACK_DMAS = LINEAR_DMAS + 2 * (len(Q_RUNS) + len(K_RUNS))

W_QL, W_KL, W_VL, W_OL, W_Q, W_QR, W_K, W_KR, W_V, W_O = (i * D for i in range(10))
C_EYE, C_HEAD, C_RANK = 0, P, P + H
C_WIDTH = C_RANK + NT * E

STEPS = [(qb, kt, kt == 0, kt == 4 * qb + 3) for qb in range(2) for kt in range(4 * qb + 4)]
"""Steps of the softmax attention of a group of heads: (query half, key tile, first, last)."""
NS = len(STEPS)
ATT = G * NS
UNITS = 2 * E * HT
CHUNKS = G * NT


def score_pieces():
    out = []
    for qt in range(NT):
        if qt >= 4:
            out += [(qt, (j,), 0, HALF, False, 0) for j in range(J)]
        n = (qt % 4 + 1) * P
        per = HALF // n
        out += [(qt, tuple(range(j, min(j + per, J))), (qt // 4) * HALF, n, True, 1) for j in range(0, J, per)]
    return out


PIECES = score_pieces()
NPC = len(PIECES) + 1

L_TURN, L_OT, L_WO, L_SUM, L_SQ, L_RMS, L_RSB, L_NRM, L_NT, L_ROUTER = 1, 2, 4, 5, 7, 8, 9, 10, 12, 14
SPLIT_AT = (2, 4)
L_LOWER, L_ROUTE, L_ROUTE2, L_GAP, L_WEIGHTS = 15, 17, 20, 23, 26
E_TURN, E_OT, E_WO, E_BIAS, E_STATS, E_AGG, E_RSA, E_RSB, E_MS, E_MSB, E_X1, E_NRM, E_NT = (
    0, 2, 3, 4, 6, 6, 7, 8, 9, 10, 11, 12, 13)
E_ROPE, E_V, E_MAX = 14, 18, 26
A_JOBS = (32, 33, 34, 36, 38, 39, 40, 41, 44, 45, 46)
A_EXP, A_MAX0, A_PHI = 42, 43, 43
E_EARLY = 3
MAX_IN_EXPERTS = 63
A_MAX, MAX_ATT_STEPS = 2, 28
E_FINAL, F_STEPS = 30, 5


def max_plan():
    where = [("experts", n, MAX_IN_EXPERTS * (n - E_MAX + 1) / (UNITS - E_MAX)) for n in range(E_MAX, UNITS)]
    rest = G * len(PIECES) - MAX_IN_EXPERTS
    where += [("attend", n, MAX_IN_EXPERTS + rest * (n + 1 - A_MAX) / MAX_ATT_STEPS) for n in range(A_MAX, A_JOBS[0])]
    plan, done, turn = {}, 0, None
    for phase, n, target in where:
        pieces, finished = [], None
        while done < min(target, G * len(PIECES)) and finished is None:
            g, i = divmod(done, len(PIECES))
            pieces.append((g, i))
            done += 1
            if i == len(PIECES) - 1:
                finished = g
        plan[phase, n] = (turn, pieces, finished)
        turn = finished
        if finished:
            assert phase == "attend" and n + 3 < finished * NS
    assert done == G * len(PIECES) and turn is None
    return plan


PLAN = max_plan()
NOTHING = (None, [], None)


def early_pieces(n):
    return PLAN.get(("experts", n), NOTHING)[1][:E_EARLY]


def late_pieces(n):
    return PLAN.get(("experts", n), NOTHING)[1][E_EARLY:]


def ring_plan():
    items = []
    for phase, n in [("experts", n) for n in range(UNITS)] + [("attend", n) for n in range(A_JOBS[0])]:
        turn, pieces, _ = PLAN.get((phase, n), NOTHING)
        early = E_EARLY if phase == "experts" else 0
        items += [("piece", g, i) for g, i in pieces[:early]]
        items += [("max", turn)] if turn is not None else []
        items += [("piece", g, i) for g, i in pieces[early:]]
        if phase == "attend" and n >= 2 and STEPS[(n - 2) % NS][3]:
            items.append(("out", n))
    return {item: i for i, item in enumerate(items)}


RING = ring_plan()
NR = len(RING)
BANKS = 3


def block_program(nc, x_rows, x_cols, attn_w, cols, rows, consts, consts_b, stack_rows, rope, w_router,
                  wg, wu, wd, out):
    with ExitStack() as ctx:
        def sb(name, shape, dt=F32):
            return ctx.enter_context(nc.sbuf_tensor(name, shape, dt))

        def sem(name):
            return ctx.enter_context(nc.semaphore(name))

        W = sb("W", [P, 10 * D])
        WG = sb("WG", [P, 2, E * HID], F32R)
        WU = sb("WU", [P, 2, E * HID], F32R)
        WD = sb("WD", [P, E * HT, D])
        WR = sb("WR", [P, E])
        COLS = sb("COLS", [P, 4])
        ROWSB = sb("ROWSB", [P, 3 * D])
        CST = sb("CST", [P, C_WIDTH])
        CSTB = sb("CSTB", [P, 2, P], BF16)
        ROPE = sb("ROPE", [P, 2, T])
        XT = sb("XT", [P, T])
        QS = sb("QS", [P, H // 2, T], BF16)
        KS = sb("KS", [P, H, T], BF16)
        PARTS = sb("PARTS", [P, 2, 3, HALF], BF16)
        TERMS = sb("TERMS", [P, 2, HALF])
        SRC = sb("SRC", [P, 2, HALF])
        PHI_QT = sb("PHI_QT", [P, T])
        VL = sb("VL", [P, NT, H, HD + 1])
        VS = sb("VS", [P, NT, H, HD + 1])
        STATE = sb("STATE", [P, NT, H, HD + 1])
        OCOPY = sb("OCOPY", [P, 2, HALF])
        ONORM = sb("ONORM", [P, NT, D])
        X1 = sb("X1", [P, NT, D])
        SUM = sb("SUM", [P, NT, D])
        XAT = sb("XAT", [P, T])
        XN = sb("XN", [P, 2, T], F32R)
        WORK = sb("WORK", [P, 8, HALF])
        MXP = sb("MXP", [P, 2, J, NT])
        NMAX = sb("NMAX", [P, J * NT])
        MREM = sb("MREM", [J * NT, P])
        MPARTS = sb("MPARTS", [J * NT, 3, P], BF16)
        SM = sb("SM", [P, 20, NT])
        BN = sb("BN", [P, NT, 6])
        MV = sb("MV", [P, NT, 2])
        LG = sb("LG", [P, 5, NT, E])
        CW = sb("CW", [P, NT, E])
        PS = ctx.enter_context(nc.psum_tensor("PS", [P, 8, HALF], F32))

        q_parts = nc.dram_tensor("q_parts", (H, 3, HD, T), BF16).ap()
        k_parts = nc.dram_tensor("k_parts", (H, 3, HD, T), BF16).ap()
        max_parts = nc.dram_tensor("max_parts", (3, J, T), BF16).ap()

        weights_loaded, consts_loaded, rope_loaded = sem("weights_loaded"), sem("consts_loaded"), sem("rope_loaded")
        staged = [sem(f"staged_{i}") for i in range(4)]
        weights_split, down_loaded = sem("weights_split"), sem("down_loaded")
        ones_loaded = sem("ones_loaded")
        setup_done, psum_cleared = sem("setup_done"), sem("psum_cleared")
        xt_loaded, x_loaded = sem("xt_loaded"), sem("x_loaded")
        x_used, xt_used = sem("x_used"), sem("xt_used")
        part1_done, rem_done, part2_done = sem("part1_done"), sem("rem_done"), sem("part2_done")
        parts_ready = sem("parts_ready")
        parts_stored = [sem("parts_stored_0"), sem("parts_stored_1")]
        stack_loaded = [sem(f"stack_loaded_{g}") for g in range(G)]
        proj_full, phi_exp, proj_read, phi_done = (sem("proj_full"), sem("phi_exp"), sem("proj_read"),
                                                     sem("phi_done"))
        nat_full, nat_added, nat_exp, kv_inputs = sem("nat_full"), sem("nat_added"), sem("nat_exp"), sem("kv_inputs")
        kv_full, kv_added, state_done = sem("kv_full"), sem("kv_added"), sem("state_done")
        ls_full, ls_copied, ls_masked, lpv_done = sem("ls_full"), sem("ls_copied"), sem("ls_masked"), sem("lpv_done")
        o_copied, o_turned, o_normed = sem("o_copied"), sem("o_turned"), sem("o_normed")
        lot_full, lot_copied, lwo_full = sem("lot_full"), sem("lot_copied"), sem("lwo_full")
        lnormed, lnt_full, lnt_copied = sem("lnormed"), sem("lnt_full"), sem("lnt_copied")
        sot_full, sot_copied, swo_full = sem("sot_full"), sem("sot_copied"), sem("swo_full")
        h_done, squares_done = sem("h_done"), sem("squares_done")
        snormed, snt_full, snt_copied = sem("snormed"), sem("snt_full"), sem("snt_copied")
        upper_ready, lower_ready = sem("upper_ready"), sem("lower_ready")
        rope_full, rope_read, rope_added = sem("rope_full"), sem("rope_read"), sem("rope_added")
        v_full, v_copied = sem("v_full"), sem("v_copied")
        piece_full, ring_read = sem("piece_full"), sem("ring_read")
        negmax_ready, mparts_ready, mparts_stored = sem("negmax_ready"), sem("mparts_ready"), sem("mparts_stored")
        max_loaded = [sem(f"max_loaded_{g}") for g in range(G)]
        st_full, exp_done, p_masked, pv_done = sem("st_full"), sem("exp_done"), sem("p_masked"), sem("pv_done")
        router_full, router_read, gap_ready, gap_exp = (sem("router_full"), sem("router_read"), sem("gap_ready"),
                                                       sem("gap_exp"))
        gu_full, silu_done, hid_done, y_full, y_read = (sem("gu_full"), sem("silu_done"), sem("hid_done"),
                                                        sem("y_full"), sem("y_read"))
        expert_added = sem("expert_added")
        out_ready, out_stored = sem("out_ready"), sem("out_stored")
        pool_waits, sp_waits = sem("pool_waits"), sem("sp_waits")

        def by_tile(v):
            return v.rearrange("p (t d) -> p t d", d=D)

        X, PHI_K = by_tile(XT[:, :]), by_tile(XAT[:, :])
        HROWS = by_tile(TERMS[:, :, :].rearrange("p a n -> p (a n)"))
        NRM = by_tile(SRC[:, :, :].rearrange("p a n -> p (a n)"))
        STAGE = WORK[:, 4:8, :]

        eye = CST[:, C_EYE:C_EYE + P]
        head_mask = CST[:, C_HEAD:C_HEAD + H].rearrange("p (h o) -> p h o", o=1)
        rank = CST[:, C_RANK:C_RANK + NT * E].rearrange("p (t e) -> p t e", e=E)
        eye_b, bias_b = CSTB[:, 0, :], CSTB[:, 1, :]
        hidden = WORK[:, 0:6, :].rearrange("p (s h) n -> p s h n", s=2)
        probs = WORK[:, :, :].rearrange("p (s j) n -> p s j n", s=2)
        block = ctx.enter_context(nc.Block())

        def half(n):
            return slice((n % 2) * HALF, (n % 2 + 1) * HALF)

        def tile(t):
            return slice(t * P, (t + 1) * P)

        def queries_of(at):
            qb, kt, _, _ = STEPS[at % NS]
            q0 = max(0, kt - 4 * qb) * P
            return q0, HALF - q0

        def finished_half(at):
            if at < 0 or not STEPS[at % NS][3]:
                return None
            return 8 + 2 * (at // NS) + STEPS[at % NS][0]

        def causal_steps(at):
            return sum(STEPS[a % NS][1] >= 4 * STEPS[a % NS][0] for a in range(at + 1))

        @block.sync
        def _(sp):
            def wait_then(signal, value):
                sp.wait_ge(signal, value)
                sp.sem_inc(sp_waits, 1)

            x_tiles = x_rows.rearrange("(b t p) d -> b p t d", b=B, p=P)
            x_batches = x_cols.rearrange("p (b t) -> b p t", b=B)
            out_tiles = out.rearrange("b (t p) d -> b p t d", p=P)
            q_rows = q_parts.rearrange("(g j o) i d t -> g o (i d) j t", g=G, o=2)
            k_rows = k_parts.rearrange("(g j o) i d t -> g o (i d) j t", g=G, o=2)

            def store_parts(b, which):
                for n in range(4):
                    dst = q_parts if n < 2 else k_parts
                    wait_then(parts_ready, (b * 2 + which) * 4 + n + 1)
                    for i in range(3):
                        part = i if n < 2 else 2 - i
                        sp.dma_start(dst[:, part, :, half(n)],
                                     PARTS[:, n % 2, i, :]).then_inc(parts_stored[n % 2], 16)

            def load_stacks(b, which, free):
                for slot in range(2):
                    wait_then(parts_stored[slot], 48 * ((b * 2 + which) * 2 + 3))
                for g in range(G):
                    if free is not None:
                        wait_then(*free(g))
                    for o in range(2):
                        r = 64 * o
                        for r0, i0, n in Q_RUNS:
                            sp.dma_start(QS[r + r0:r + r0 + n * HD, 2 * g:2 * g + 2, :],
                                         q_rows[g, o, i0 * HD:(i0 + n) * HD]).then_inc(stack_loaded[g], 16)
                        for r0, i0, n in K_RUNS:
                            sp.dma_start(KS[r + r0:r + r0 + n * HD, 4 * g + o:4 * g + o + 3:2, :],
                                         k_rows[g, o, i0 * HD:(i0 + n) * HD]).then_inc(stack_loaded[g], 16)
                        if which == 0:
                            sp.dma_start(QS[r + ROWS:r + ROWS + 3, 2 * g:2 * g + 2, :],
                                         stack_rows[0, :, 0:2, :]).then_inc(stack_loaded[g], 16)

            def load_max(b, g):
                u = b * G + g
                wait_then(mparts_ready, u + 1)
                sp.dma_start(max_parts.rearrange("i j (t q) -> (j t) i q", q=P),
                             MPARTS[:, :, :]).then_inc(mparts_stored, 16)
                wait_then(mparts_stored, 16 * (u + 1))
                src = max_parts.rearrange("i (j o) t -> o i j t", o=2)
                for o in range(2):
                    sp.dma_start(QS[64 * o + ROWS:64 * o + ROWS + 3, 2 * g:2 * g + 2, :],
                                 src[o]).then_inc(max_loaded[g], 16)

            def load_xt(b):
                wait_then(x_used, b)
                sp.dma_start(XT[:, :], x_batches[b]).then_inc(xt_loaded, 16)

            def load_x(b):
                wait_then(xt_used, b + 1)
                sp.dma_start(X, x_tiles[b]).then_inc(x_loaded, 16)

            def softmax_inputs(b):
                store_parts(b, 1)
                load_stacks(b, 1, lambda g: (lpv_done, (b + 1) * CHUNKS))
                load_max(b, 0)

            def attend(b):
                for g in range(1, G):
                    load_max(b, g)

            def batch(b, more):
                attend(b)
                store_parts(b + 1, 0)
                load_stacks(b + 1, 0, lambda g: (pv_done, b * ATT + (g + 1) * NS))
                load_x(b + 1)
                softmax_inputs(b + 1)
                if more:
                    load_xt(b + 2)
                store(b)

            def store(b):
                wait_then(out_ready, b + 1)
                sp.dma_start(out_tiles[b], SUM[:, :, :]).then_inc(out_stored, 16)

            sp.dma_start(XT[:, :], x_batches[0]).then_inc(xt_loaded, 16)
            sp.dma_start(W[:, :], attn_w).then_inc(weights_loaded, 16)
            sp.dma_start(COLS[:, :], cols).then_inc(weights_loaded, 16)
            sp.dma_start(ROWSB[:, :], rows).then_inc(consts_loaded, 16)
            sp.dma_start(CST[:, :], consts).then_inc(consts_loaded, 16)
            sp.dma_start(CSTB[:, :, :], consts_b.rearrange("a p n -> p a n")).then_inc(consts_loaded, 16)
            sp.dma_start(WR[:, :], w_router).then_inc(consts_loaded, 16)
            store_parts(0, 0)
            sp.wait_ge(setup_done, 1)
            sp.dma_start(KS[ROWS:ROWS + 3, 0:H:2, :], stack_rows[1]).then_inc(ones_loaded, 16)
            sp.dma_start(KS[64 + ROWS:64 + ROWS + 3, 1:H:2, :], stack_rows[1]).then_inc(ones_loaded, 16)
            load_stacks(0, 0, None)
            sp.dma_start(ROPE[:, :, :], rope.rearrange("a p t -> p a t")).then_inc(rope_loaded, 16)
            load_x(0)
            sp.dma_start(WD[:, :, :], wd.rearrange("e (t p) d -> p (e t) d", p=P)).then_inc(down_loaded, 16)
            softmax_inputs(0)
            load_xt(1)
            with sp.Fori(0, B - 2) as b:
                batch(b, True)
            batch(B - 2, False)
            attend(B - 1)
            store(B - 1)
            sp.wait_ge(out_stored, 16 * B + 16)

        @block.tensor
        def _(pe):
            def project(b, r, first):
                bank = 5 + r % 2
                if r < 4:
                    if r == 0:
                        pe.wait_ge(xt_loaded, 16 * (b + 1))
                        if not first:
                            pe.wait_ge(ring_read, b * NR)
                    if r >= 2:
                        pe.wait_ge(proj_read, b * 4 + r - 1)
                    w = W[:, W_QL:W_QL + D] if r < 2 else W[:, W_KL:W_KL + D]
                    nc.tensor.matmul(PS[:, bank, :], w, XT[:, half(r)], start=True, stop=True).then_inc(proj_full, 1)
                elif r < 8:
                    if r < 6:
                        pe.wait_ge(proj_read, b * 4 + r - 1)
                    else:
                        pe.wait_ge(nat_added, b * 4 + r - 5)
                    for m in range(2):
                        last = nc.tensor.matmul(PS[:, bank, m * 256:m * 256 + 256], XT[:, tile(2 * (r - 4) + m)],
                                                W[:, W_KL:W_KL + 2 * D], start=True, stop=True)
                    last.then_inc(nat_full, 1)
                else:
                    if r == 8:
                        pe.wait_ge(kv_inputs, b + 1)
                        pe.sem_inc(xt_used, 1)
                    if r == 10:
                        pe.wait_ge(kv_added, b * 3 + 1)
                    tiles = range(3 * (r - 8), min(3 * (r - 8) + 3, NT - 1))
                    for m, t in enumerate(tiles):
                        last = nc.tensor.matmul(PS[:, bank, m * 144:m * 144 + 144], PHI_K[:, t, :],
                                                VL[:, t, :, :], start=True, stop=True)
                    last.then_inc(kv_full, 1)

            def linear_scores(b, n):
                g, c = n // NT, n % NT
                if c == 0:
                    pe.wait_ge(stack_loaded[g], 16 * (b * STACK_DMAS + LINEAR_DMAS))
                if n >= 3:
                    pe.wait_ge(ls_copied, b * CHUNKS + n - 2)
                for j in range(J):
                    last = nc.tensor.matmul(PS[:, n % 3, j * P:(j + 1) * P], KS[:, 4 * g + j, tile(c)],
                                            QS[:, 2 * g + j // 2, tile(c)], start=True, stop=True)
                last.then_inc(ls_full, 1)

            def linear_outputs(b, n, first):
                g, c = n // NT, n % NT
                u = n // 4
                cols = slice((c % 4) * P, (c % 4 + 1) * P)
                pe.wait_ge(ls_masked, b * CHUNKS + n + 1)
                if c % 4 == 0:
                    if u >= 2:
                        pe.wait_ge(o_copied, b * 16 + u - 1)
                    elif u == 0 and not first:
                        pe.wait_ge(o_copied, b * 16)
                for j in range(J):
                    last = nc.tensor.matmul(PS[32 * j:32 * j + HD + 1, 4 + u % 2, cols], VL[:, c, 4 * g + j, :],
                                            WORK[:, n % 4, tile(j)], start=True, stop=(c == 0),
                                            tile_position=(0, 32 * j))
                if c:
                    for j in range(J):
                        last = nc.tensor.matmul(PS[32 * j:32 * j + HD + 1, 4 + u % 2, cols],
                                                STATE[:, c, 4 * g + j, :], PHI_QT[:, tile(c)],
                                                start=False, stop=True, tile_position=(0, 32 * j))
                last.then_inc(lpv_done, 1)

            def turn_outputs(b, u, item=None):
                pe.wait_ge(o_copied, b * 16 + u + 1)
                if item is None:
                    pe.wait_ge(o_normed, b * 16 + u + 1)
                bank = 7 if item is None else ring_bank(b, item)
                for t in range(4):
                    last = nc.tensor.transpose(PS[:, bank, tile(t)], OCOPY[:, u % 2, tile(t)], eye)
                last.then_inc(o_turned, 1)

            def turn_rows(src, banks, full):
                for t in range(NT):
                    last = nc.tensor.transpose(PS[:, banks[t // 4], tile(t % 4)], src[:, t, :], eye)
                    if t % 4 == 3:
                        last.then_inc(full, 1)

            def rows_times(src, w, banks, full):
                for t in range(NT):
                    last = nc.tensor.matmul(PS[:, banks[t // 4], tile(t % 4)], src[:, tile(t)], w,
                                            start=True, stop=True)
                    if t % 4 == 3:
                        last.then_inc(full, 1)

            def soft_output(b, n):
                if n == L_TURN:
                    turn_outputs(b, 15)
                if n == L_OT:
                    pe.wait_ge(o_normed, b * 16 + 17)
                    turn_rows(ONORM, (3, 6), sot_full)
                if n == L_WO:
                    pe.wait_ge(sot_copied, b * 2 + 2)
                    rows_times(XAT, W[:, W_O:W_O + D], (3, 6), swo_full)
                if n == L_NT:
                    pe.wait_ge(snormed, b + 1)
                    turn_rows(NRM, (3, 6), snt_full)
                if n == L_ROUTER:
                    pe.wait_ge(snt_copied, b * 2 + 2)
                    for t in range(NT):
                        last = nc.tensor.matmul(PS[:, 6, t * E:(t + 1) * E], XAT[:, tile(t)], WR[:, :],
                                                start=True, stop=True)
                    last.then_inc(router_full, 1)

            def ring_bank(b, item):
                idx = RING[item]
                if idx >= BANKS:
                    pe.wait_ge(ring_read, b * NR + idx - BANKS + 1)
                return 5 + idx % BANKS

            def max_pieces(b, pieces):
                for g, i in pieces:
                    qt, heads, k0, n, causal, _ = PIECES[i]
                    if i == 0:
                        pe.wait_ge(stack_loaded[g], 16 * (b * STACK_DMAS + STACK_DMAS))
                        if g == 0:
                            pe.wait_ge(v_copied, b + 1)
                    bank = ring_bank(b, ("piece", g, i))
                    for m, j in enumerate(heads):
                        last = nc.tensor.matmul(PS[:, bank, m * n:(m + 1) * n], QS[:, 2 * g + j // 2, tile(qt)],
                                                KS[:, 4 * g + j, k0:k0 + n], start=True, stop=not causal)
                        if causal:
                            last = nc.tensor.matmul(PS[:, bank, (m + 1) * n - P:(m + 1) * n], eye_b, bias_b,
                                                    start=False, stop=True)
                    last.then_inc(piece_full, 1)

            def turn_max(b, g):
                if g is None:
                    return
                pe.wait_ge(negmax_ready, b * G + g + 1)
                bank = ring_bank(b, ("max", g))
                nc.tensor.transpose(PS[0:J * NT, bank, 0:P], NMAX[:, :], eye).then_inc(piece_full, 1)

            def prepare(b, n, first):
                if n == E_TURN:
                    turn_outputs(b, 7)
                if n == E_OT:
                    pe.wait_ge(o_normed, b * 16 + 9)
                    if not first:
                        pe.wait_ge(router_read, b)
                    turn_rows(ONORM, (5, 6), lot_full)
                if n == E_WO:
                    pe.wait_ge(lot_copied, b * 2 + 2)
                    rows_times(XAT, W[:, W_OL:W_OL + D], (5, 6), lwo_full)
                if n == E_NT:
                    pe.wait_ge(lnormed, b + 1)
                    turn_rows(NRM, (5, 6), lnt_full)
                if E_ROPE <= n < E_ROPE + 4:
                    m = n - E_ROPE
                    if m == 0:
                        pe.wait_ge(lnt_copied, b * 2 + 2)
                    else:
                        pe.wait_ge(rope_read, b * 4 + m)
                    w, wr = (W_Q, W_QR) if m < 2 else (W_K, W_KR)
                    nc.tensor.matmul(PS[:, 5, :], W[:, w:w + D], XAT[:, half(m)], start=True, stop=True)
                    nc.tensor.matmul(PS[:, 6, :], W[:, wr:wr + D], XAT[:, half(m)],
                                     start=True, stop=True).then_inc(rope_full, 1)
                if n == E_V:
                    pe.wait_ge(rope_read, b * 4 + 4)
                    rows_times(XAT, W[:, W_V:W_V + D], (5, 6), v_full)
                if first:
                    max_pieces(b, early_pieces(n))
                turn_max(b, PLAN.get(("experts", n), NOTHING)[0])
                max_pieces(b, late_pieces(n))

            def scores(b, at, pair):
                g, (qb, kt, _, _) = at // NS, STEPS[at % NS]
                q0, n = queries_of(at)
                if at:
                    pe.wait_ge(exp_done, b * 2 * ATT + 2 * (at - 1) + pair + 1)
                for m in range(2):
                    last = nc.tensor.matmul(PS[:, 2 * pair + m, 0:n], KS[:, 4 * g + 2 * pair + m, tile(kt)],
                                            QS[:, 2 * g + pair, qb * HALF + q0:(qb + 1) * HALF],
                                            start=True, stop=True)
                last.then_inc(st_full, 1)

            def values(b, at):
                g, (qb, kt, first, final) = at // NS, STEPS[at % NS]
                q0, n = queries_of(at)
                pe.wait_ge(exp_done, b * 2 * ATT + 2 * at + 2)
                if kt >= 4 * qb:
                    pe.wait_ge(p_masked, b * 2 * causal_steps(ATT - 1) + 2 * causal_steps(at))
                if first:
                    if at == 0:
                        pe.wait_ge(y_read, b * 2 * E + 2 * E)
                    else:
                        pe.wait_ge(o_copied, b * 16 + 8 + 2 * g + qb)
                for j in range(J):
                    last = nc.tensor.matmul(PS[32 * j:32 * j + HD + 1, 4, q0:HALF], VS[:, kt, 4 * g + j, :],
                                            probs[:, at % 2, j, 0:n], start=first, stop=final,
                                            tile_position=(0, 32 * j))
                last.then_inc(pv_done, 1)

            def attend(b, beside):
                for at in range(ATT):
                    if at % NS == 0:
                        pe.wait_ge(max_loaded[at // NS], 32 * (b + 1))
                    turn, pieces, _ = PLAN.get(("attend", at), NOTHING)
                    scores(b, at, 0)
                    early = 0 if turn is not None else (len(pieces) + 1) // 3
                    late = 0 if turn is not None else early + (len(pieces) - early + 1) // 2
                    max_pieces(b, pieces[:early])
                    scores(b, at, 1)
                    max_pieces(b, pieces[early:late])
                    if at:
                        values(b, at - 1)
                    turn_max(b, turn)
                    max_pieces(b, pieces[late:])
                    if finished_half(at - 2) is not None:
                        turn_outputs(b, finished_half(at - 2), ("out", at) if ("out", at) in RING else None)
                    if beside and at in A_JOBS:
                        project(b + 1, A_JOBS.index(at), False)
                values(b, ATT - 1)

            def gate_up(b, n, pieces):
                tb, e, ht = n // (E * HT), n // HT % E, n % HT
                if n >= 2:
                    pe.wait_ge(silu_done, b * UNITS + n - 1)
                bank = 2 * (n % 2)
                cols = slice(e * HID + ht * P, e * HID + (ht + 1) * P)
                for w, dst in ((WG, bank), (WU, bank + 1)):
                    if w is WU:
                        max_pieces(b + 1, pieces[:1])
                        if n >= 2:
                            pe.wait_ge(hid_done, b * UNITS + n - 1)
                    for i, (a, c) in enumerate(((0, 0), (0, 1), (1, 0))):
                        last = nc.tensor.matmul(PS[:, dst, :], w[:, a, cols], XN[:, c, half(tb)],
                                                start=(i == 0), stop=(i == 2))
                last.then_inc(gu_full, 1)
                max_pieces(b + 1, pieces[1:])

            def down(b, m):
                pe.wait_ge(hid_done, b * UNITS + 3 * m + 3)
                pe.wait_ge(y_read, b * 2 * E + 2 * E + m)
                for t in range(4):
                    for ht in range(HT):
                        last = nc.tensor.matmul(PS[:, 4, tile(t)], hidden[:, m % 2, ht, tile(t)],
                                                WD[:, (m % E) * HT + ht, :], start=(ht == 0), stop=(ht == HT - 1))
                last.then_inc(y_full, 1)

            def linear(b, soft):
                pe.wait_ge(state_done, b + 1)
                for n in range(CHUNKS):
                    linear_scores(b, n)
                    if n >= 2:
                        linear_outputs(b, n - 2, not soft)
                    if n % 4 == 3 and n > 4:
                        turn_outputs(b, n // 4 - 1)
                    if soft:
                        soft_output(b - 1, n)
                linear_outputs(b, CHUNKS - 2, not soft)
                linear_outputs(b, CHUNKS - 1, not soft)

            def experts(b, beside):
                pe.wait_ge(lower_ready, b + 1)
                for n in range(UNITS):
                    gate_up(b, n, early_pieces(n) if beside else [])
                    if n % HT == 1 and n > HT:
                        down(b, n // HT - 1)
                    if beside:
                        prepare(b + 1, n, False)
                down(b, 2 * E - 1)

            pe.wait_ge(psum_cleared, 1)
            pe.wait_ge(weights_loaded, 16 * 2)
            for r in range(len(A_JOBS)):
                project(0, r, True)
            pe.wait_ge(ones_loaded, 32)
            pe.wait_ge(consts_loaded, 16 * 4)
            linear(0, False)
            for n in range(UNITS):
                prepare(0, n, True)
            pe.wait_ge(weights_split, 2 * E)
            pe.wait_ge(down_loaded, 16)
            with pe.Fori(0, B - 1) as b:
                attend(b, True)
                linear(b + 1, True)
                experts(b, True)
            attend(B - 1, False)
            for n in (L_TURN, L_OT, L_WO, L_NT, L_ROUTER):
                soft_output(B - 1, n)
            experts(B - 1, False)

        @block.scalar
        def _(act):
            def part(b, n, second):
                job = (b - 1) * 4 + n
                if second:
                    act.wait_ge(rem_done, job + 1)
                    nc.scalar.copy(PARTS[:, n % 2, 1, :], SRC[:, n % 2, :]).then_inc(part2_done, 1)
                else:
                    act.wait_ge(rope_added, job + 1)
                    act.wait_ge(parts_stored[n % 2], 48 * ((b * 2 + 1) * 2 + n // 2 + 1))
                    nc.scalar.copy(PARTS[:, n % 2, 0, :], SRC[:, n % 2, :]).then_inc(part1_done, 1)

            def project(b, r):
                if r < 4:
                    act.wait_ge(proj_full, b * 4 + r + 1)
                    if r >= 2:
                        act.wait_ge(phi_done, b * 4 + r - 1)
                    nc.scalar.activation(TERMS[:, r % 2, :], PS[:, 5 + r % 2, :], ACT.Exp,
                                         bias=COLS[:, r // 2:r // 2 + 1]).then_inc(phi_exp, 1)

            def natural_exp(b):
                act.wait_ge(nat_added, b * 4 + 4)
                nc.scalar.activation(NRM, PHI_K, ACT.Exp).then_inc(nat_exp, 1)

            def copy_outputs(u, bank):
                nc.scalar.copy(OCOPY[:, u % 2, :], PS[:, bank, :]).then_inc(o_copied, 1)

            def copy_turned(b, dst, banks, full, done, scale=None):
                for n in range(2):
                    act.wait_ge(full, b * 2 + n + 1)
                    if scale is None:
                        nc.scalar.copy(dst[:, half(n)], PS[:, banks[n], :]).then_inc(done, 1)
                    else:
                        nc.scalar.activation(dst[:, half(n)], PS[:, banks[n], :], ACT.Copy,
                                             scale=scale).then_inc(done, 1)

            def soft_output(b, n):
                if n == L_OT:
                    copy_turned(b, XAT, (3, 6), sot_full, sot_copied)
                if n == L_SQ:
                    act.wait_ge(h_done, b + 1)
                    nc.scalar.activation(NRM, HROWS, ACT.Square).then_inc(squares_done, 1)
                if n == L_NT:
                    copy_turned(b, XAT, (3, 6), snt_full, snt_copied, COLS[:, 3:4])
                    act.wait_ge(snt_copied, b * 2 + 2)
                    nc.scalar.copy(XN[:, 0, :], XAT[:, :]).then_inc(upper_ready, 1)
                if n == L_GAP:
                    act.wait_ge(gap_ready, b + 1)
                    nc.scalar.activation(SM[:, 5, :], SM[:, 4, :], ACT.Exp).then_inc(gap_exp, 1)

            def linear(b, soft):
                for n in range(CHUNKS):
                    act.wait_ge(ls_full, b * CHUNKS + n + 1)
                    if n >= 4:
                        act.wait_ge(lpv_done, b * CHUNKS + n - 3)
                    nc.scalar.copy(WORK[:, n % 4, :], PS[:, n % 3, :]).then_inc(ls_copied, 1)
                    if n % 4 == 1 and n > 4:
                        act.wait_ge(lpv_done, b * CHUNKS + n - 1)
                        copy_outputs(n // 4 - 1, 4 + (n // 4 - 1) % 2)
                    if soft:
                        soft_output(b - 1, n)
                act.wait_ge(lpv_done, b * CHUNKS + CHUNKS)
                copy_outputs(7, 5)

            def prepare(b, n, first):
                if n == E_OT:
                    copy_turned(b, XAT, (5, 6), lot_full, lot_copied)
                if n == E_NT:
                    copy_turned(b, XAT, (5, 6), lnt_full, lnt_copied, COLS[:, 2:3])
                if E_ROPE < n <= E_ROPE + 4 and not first:
                    part(b, n - E_ROPE - 1, False)
                if E_ROPE + 1 < n <= E_ROPE + 5 and not first:
                    part(b, n - E_ROPE - 2, True)
                if n == E_V:
                    act.wait_ge(v_full, b * 2 + 2)
                    for m in range(2):
                        last = nc.scalar.copy(VS[:, 4 * m:4 * m + 4, :, 0:HD],
                                              PS[:, 5 + m, :].rearrange("p (t h e) -> p t h e", t=4, h=H))
                    last.then_inc(v_copied, 1)

            def attend(b, beside):
                for at in range(ATT):
                    _, n = queries_of(at)
                    for pair in range(2):
                        act.wait_ge(st_full, b * 2 * ATT + 2 * at + pair + 1)
                        if at >= 2 and pair == 0:
                            act.wait_ge(pv_done, b * G * NS + at - 1)
                        nc.scalar.activation(probs[:, at % 2, 2 * pair:2 * pair + 2, 0:n],
                                             PS[:, 2 * pair:2 * pair + 2, 0:n], ACT.Exp,
                                             scale=SCALE).then_inc(exp_done, 1)
                    if finished_half(at - 1) is not None:
                        act.wait_ge(pv_done, b * G * NS + at)
                        copy_outputs(finished_half(at - 1), 4)
                    if beside and at in A_JOBS:
                        project(b + 1, A_JOBS.index(at))
                    if beside and at == A_EXP:
                        natural_exp(b + 1)
                act.wait_ge(pv_done, b * G * NS + ATT)
                copy_outputs(15, 4)

            def weigh_expert(b, m):
                tb, e = m // E, m % E
                act.wait_ge(y_full, b * 2 * E + m + 1)
                act.wait_ge(expert_added, b * 2 * E + 2 * E + m - 1)
                for t in range(4):
                    last = nc.scalar.activation(OCOPY[:, m % 2, tile(t)], PS[:, 4, tile(t)], ACT.Copy,
                                                scale=CW[:, 4 * tb + t, e:e + 1])
                last.then_inc(y_read, 1)

            def experts(b, beside):
                for n in range(UNITS):
                    act.wait_ge(gu_full, b * UNITS + n + 1)
                    if n >= 2:
                        act.wait_ge(hid_done, b * UNITS + n - 1)
                    nc.scalar.activation(WORK[:, 6 + n % 2, :], PS[:, 2 * (n % 2), :], ACT.Silu).then_inc(silu_done, 1)
                    if beside:
                        prepare(b + 1, n, False)
                    elif n == 2:
                        soft_output(b, L_GAP)
                    if n % HT == 2 and n > HT:
                        weigh_expert(b, n // HT - 1)
                weigh_expert(b, 2 * E - 1)

            act.wait_ge(weights_loaded, 16 * 2)
            for r in range(4):
                project(0, r)
            natural_exp(0)
            linear(0, False)
            for n in range(UNITS):
                prepare(0, n, True)
            with act.Fori(0, B - 1) as b:
                attend(b, True)
                linear(b + 1, True)
                experts(b, True)
            attend(B - 1, False)
            for n in (L_OT, L_SQ, L_NT):
                soft_output(B - 1, n)
            experts(B - 1, False)

        @block.gpsimd
        def _(pool):
            def wait_then(signal, value):
                pool.wait_ge(signal, value)
                pool.sem_inc(pool_waits, 1)

            def rest(b, n, second):
                job = (b - 1) * 4 + n
                if second:
                    pool.wait_ge(part2_done, job + 1)
                    nc.gpsimd.tensor_tensor(PARTS[:, n % 2, 2, :], SRC[:, n % 2, :], PARTS[:, n % 2, 1, :],
                                            ALU.subtract).then_inc(parts_ready, 1)
                else:
                    pool.wait_ge(part1_done, job + 1)
                    nc.gpsimd.tensor_tensor(SRC[:, n % 2, :], SRC[:, n % 2, :], PARTS[:, n % 2, 0, :],
                                            ALU.subtract).then_inc(rem_done, 1)

            def causal(v, heads, done):
                pool.affine_select(out=v, in_=v, compare_op=ALU.is_ge, fill=0.0, base=0,
                                   pattern=[[0, heads], [1, P]], channel_multiplier=-1).then_inc(done, 1)

            def linear(b):
                for n in range(CHUNKS):
                    wait_then(ls_copied, b * CHUNKS + n + 1)
                    causal(WORK[:, n % 4, :].rearrange("p (j q) -> p j q", j=J), J, ls_masked)

            def prepare(b, n):
                if 2 <= n < 6:
                    rest(b, n - 2, True)
                if n < 4:
                    pool.wait_ge(rope_read, b * 4 + n + 1)
                    if n >= 2:
                        pool.wait_ge(parts_ready, (b * 2 + 1) * 4 + n - 1)
                    nc.gpsimd.tensor_tensor(SRC[:, n % 2, :], TERMS[:, 0, :], TERMS[:, 1, :],
                                            ALU.add).then_inc(rope_added, 1)
                if 1 <= n < 5:
                    rest(b, n - 1, False)

            def experts(b, beside):
                for n in range(UNITS):
                    if beside and E_ROPE <= n < E_ROPE + 6:
                        prepare(b + 1, n - E_ROPE)
                    if n % HT == 2 and n > HT:
                        add_expert(b, n // HT - 1)
                add_expert(b, 2 * E - 1)

            def add_expert(b, m):
                tb = m // E
                rows = SUM[:, 4 * tb:4 * tb + 4, :]
                pool.wait_ge(y_read, b * 2 * E + 2 * E + m + 1)
                pool.wait_ge(expert_added, b * 2 * E + 2 * E + m)
                nc.gpsimd.tensor_tensor(rows, rows, by_tile(OCOPY[:, m % 2, :]), ALU.add).then_inc(expert_added, 1)

            def attend(b):
                for at in range(ATT):
                    qb, kt, _, _ = STEPS[at % NS]
                    if kt >= 4 * qb:
                        for pair in range(2):
                            wait_then(exp_done, b * 2 * ATT + 2 * at + pair + 1)
                            causal(probs[:, at % 2, 2 * pair:2 * pair + 2, 0:P], 2, p_masked)

            def stage_weights(e):
                if e >= 4:
                    pool.wait_ge(weights_split, e - 3)
                pool.dma_start(STAGE[:, e % 4, 0:HID], (wg if e < E else wu)[e % E]).then_inc(staged[e % 4], 16)

            pool.memset(QS[:, :, :], 0.0)
            pool.memset(KS[:, :, :], 0.0)
            pool.drain().then_inc(setup_done, 1)
            for e in range(4):
                stage_weights(e)
            linear(0)
            for e in range(4, 2 * E):
                stage_weights(e)
            with pool.Fori(0, B - 1) as b:
                attend(b)
                linear(b + 1)
                experts(b, True)
            attend(B - 1)
            experts(B - 1, False)

        @block.vector
        def _(dve):
            def seed(y, v):
                nc.vector.tensor_scalar(y.bitcast(I32), v.bitcast(I32), -0.5, float(0x5F3759DF), ALU.mult, ALU.add)
                dve.drain()

            def newton(y, v, t):
                nc.vector.tensor_tensor(t, y, y, ALU.mult)
                dve.drain()
                nc.vector.scalar_tensor_tensor(t, t, -0.5, v, ALU.mult, ALU.mult)
                dve.drain()
                nc.vector.scalar_tensor_tensor(y, t, 1.5, y, ALU.add, ALU.mult)
                dve.drain()

            def wide(v, n):
                return v.rearrange("p (t o) -> p t o", o=1).to_broadcast([P, NT, n])

            def four(t, n):
                return t[:, 4 * n:4 * n + 4, :]

            def rows_of(bank):
                return PS[:, bank, :].rearrange("p (t d) -> p t d", d=D)

            def split(b, which, n):
                src = PHI_QT[:, half(n)] if which == 0 and n < 2 else SRC[:, n % 2, :]
                parts, rem = PARTS[:, n % 2], SRC[:, n % 2, :]
                dve.wait_ge(parts_stored[n % 2], 48 * ((b * 2 + which) * 2 + n // 2 + 1))
                nc.vector.tensor_copy(parts[:, 0, :], src)
                dve.drain()
                nc.vector.tensor_tensor(rem, src, parts[:, 0, :], ALU.subtract)
                dve.drain()
                nc.vector.tensor_copy(parts[:, 1, :], rem)
                dve.drain()
                nc.vector.tensor_tensor(parts[:, 2, :], rem, parts[:, 1, :], ALU.subtract)
                dve.drain().then_inc(parts_ready, 1)

            def project(b, r):
                bank = 5 + r % 2
                if r < 4:
                    phi = PHI_QT[:, half(r)] if r < 2 else SRC[:, r % 2, :]
                    dve.wait_ge(phi_exp, b * 4 + r + 1)
                    nc.vector.tensor_scalar(phi, PS[:, bank, :], COLS[:, r // 2:r // 2 + 1], 0.0, ALU.add, ALU.max)
                    dve.drain().then_inc(proj_read, 1)
                    nc.vector.scalar_tensor_tensor(phi, TERMS[:, r % 2, :], 1.0, phi, ALU.min, ALU.add)
                    dve.drain().then_inc(phi_done, 1)
                elif r < 8:
                    dve.wait_ge(nat_full, b * 4 + r - 3)
                    for m in range(2):
                        t = 2 * (r - 4) + m
                        src = PS[:, bank, m * 256:m * 256 + 256]
                        nc.vector.tensor_tensor(PHI_K[:, t, :], src[:, 0:D], ROWSB[:, 0:D], ALU.add)
                        nc.vector.tensor_tensor(VL[:, t, :, 0:HD], src[:, D:2 * D].rearrange("p (h e) -> p h e", h=H),
                                                ROWSB[:, D:2 * D].rearrange("p (h e) -> p h e", h=H), ALU.add)
                    dve.drain().then_inc(nat_added, 1)
                else:
                    dve.wait_ge(kv_full, b * 3 + r - 7)
                    for m, t in enumerate(range(3 * (r - 8), min(3 * (r - 8) + 3, NT - 1))):
                        src = PS[:, bank, m * 144:m * 144 + 144].rearrange("p (h e) -> p h e", h=H)
                        nc.vector.tensor_tensor(STATE[:, t + 1, :, :], src, head_mask.to_broadcast([P, H, HD + 1]),
                                                ALU.mult)
                        dve.drain()
                        if t:
                            nc.vector.tensor_tensor(STATE[:, t + 1, :, :], STATE[:, t + 1, :, :], STATE[:, t, :, :],
                                                    ALU.add)
                            dve.drain()
                    dve.drain().then_inc(kv_added, 1)
                    if r == 10:
                        dve.sem_inc(state_done, 1)
                if 1 <= r < 5:
                    split(b, 0, r - 1)

            def natural_relu(b):
                dve.wait_ge(nat_exp, b + 1)
                nc.vector.tensor_scalar(PHI_K, PHI_K, 0.0, None, ALU.max)
                dve.drain()

            def natural_phi():
                nc.vector.scalar_tensor_tensor(PHI_K, NRM, 1.0, PHI_K, ALU.min, ALU.add)
                dve.drain().then_inc(kv_inputs, 1)

            def norm_outputs(b, u, eps, item=None):
                g, qb = u % 8 // 2, u % 2
                bank = 7 if item is None else 5 + RING[item] % BANKS
                src = PS[:, bank, :].rearrange("p (t j c) -> p t j c", t=4, j=J)
                den = SM[:, 6:8, :].rearrange("p a b -> p (a b)").rearrange("p (t j o) -> p t j o", t=4, o=1)
                dve.wait_ge(o_turned, b * 16 + u + 1)
                if eps:
                    nc.vector.tensor_scalar(den, src[:, :, :, HD:HD + 1], eps, None, ALU.add)
                    dve.drain()
                    nc.vector.reciprocal(den, den)
                else:
                    nc.vector.reciprocal(den, src[:, :, :, HD:HD + 1])
                dve.drain()
                nc.vector.tensor_tensor(
                    ONORM[:, 4 * qb:4 * qb + 4, g * 32:g * 32 + 32].rearrange("p t (j e) -> p t j e", j=J),
                    src[:, :, :, 0:HD], den.to_broadcast([P, 4, J, HD]), ALU.mult)
                dve.drain().then_inc(o_normed, 1)
                if item is not None:
                    dve.sem_inc(ring_read, 1)

            def layer_stats(src, tiles):
                for t in tiles:
                    nc.vector.bn_stats(BN[:, t, :], src[:, t, :])
                dve.drain()

            def layer_variance(var, tiles):
                for t in tiles:
                    nc.vector.bn_aggr(MV[:, t, :], BN[:, t, :])
                dve.drain()
                nc.vector.tensor_scalar(var, MV[:, tiles[0]:tiles[-1] + 1, 1], LN_EPS, None, ALU.add)
                dve.drain()

            def layer_apply(dst, src, rstd, tiles):
                for t in tiles:
                    nc.vector.tensor_scalar(dst[:, t, :], src[:, t, :], MV[:, t, 0:1], rstd[:, t:t + 1],
                                            ALU.subtract, ALU.mult)
                dve.drain()

            def prepare(b, n, first):
                var, rstd, tmp, ms, rms = (SM[:, i, :] for i in range(14, 19))
                if n == E_TURN:
                    norm_outputs(b, 7, LIN_EPS)
                if n == E_WO:
                    dve.wait_ge(x_loaded, 16 * (b + 1))
                    for m in range(2):
                        dve.wait_ge(lwo_full, b * 2 + m + 1)
                        nc.vector.tensor_tensor(four(X1, m), rows_of(5 + m), four(X, m), ALU.add)
                    dve.drain().then_inc(x_used, 1)
                if n == E_BIAS:
                    nc.vector.tensor_tensor(X1[:, :, :], X1[:, :, :],
                                            ROWSB[:, 2 * D:3 * D].rearrange("p (o d) -> p o d", o=1).to_broadcast([P, NT, D]),
                                            ALU.add)
                    dve.drain()
                if n == E_STATS:
                    layer_stats(X1, range(NT))
                if n == E_AGG:
                    layer_variance(var, range(NT))
                if n == E_RSA:
                    seed(rstd, var)
                    newton(rstd, var, tmp)
                if n == E_RSB:
                    newton(rstd, var, tmp)
                    newton(rstd, var, tmp)
                if n == E_MS:
                    nc.vector.tensor_tensor(tmp, rstd, rstd, ALU.mult)
                    dve.drain()
                    nc.vector.tensor_tensor(ms, tmp, MV[:, :, 1], ALU.mult)
                    dve.drain()
                    nc.vector.tensor_scalar(ms, ms, RMS_EPS, None, ALU.add)
                    dve.drain()
                    seed(rms, ms)
                    newton(rms, ms, tmp)
                if n == E_MSB:
                    newton(rms, ms, tmp)
                    newton(rms, ms, tmp)
                if n == E_X1:
                    layer_apply(X1, X1, rstd, range(NT))
                if n == E_NRM:
                    nc.vector.tensor_tensor(NRM, X1[:, :, :], wide(rms, D), ALU.mult).then_inc(lnormed, 1)
                if E_ROPE <= n < E_ROPE + 4:
                    m = n - E_ROPE
                    dve.wait_ge(rope_full, b * 4 + m + 1)
                    if m and not first:
                        dve.wait_ge(rope_added, (b - 1) * 4 + m)
                    nc.vector.tensor_tensor(TERMS[:, 0, :], PS[:, 5, :], ROPE[:, 0, half(m)], ALU.mult)
                    nc.vector.tensor_tensor(TERMS[:, 1, :], PS[:, 6, :], ROPE[:, 1, half(m)],
                                            ALU.mult).then_inc(rope_read, 1)
                    if first:
                        dve.drain()
                        nc.vector.tensor_tensor(SRC[:, m % 2, :], TERMS[:, 0, :], TERMS[:, 1, :], ALU.add)
                        dve.drain()
                        split(b, 1, m)
                turn, _, finished = PLAN.get(("experts", n), NOTHING)
                if first:
                    maxima(b, None, early_pieces(n), None)
                maxima(b, turn, late_pieces(n), finished)

            def maxima(b, turned, pieces, finished):
                if turned is not None:
                    idx = turned * NPC + NPC - 1
                    src = PS[0:J * NT, 5 + RING["max", turned] % BANKS, 0:P]
                    dve.wait_ge(piece_full, b * G * NPC + idx + 1)
                    nc.vector.tensor_copy(MPARTS[:, 0, :], src)
                    dve.drain()
                    nc.vector.tensor_tensor(MREM[:, :], src, MPARTS[:, 0, :], ALU.subtract)
                    dve.drain().then_inc(ring_read, 1)
                    nc.vector.tensor_copy(MPARTS[:, 1, :], MREM[:, :])
                    dve.drain()
                    nc.vector.tensor_tensor(MPARTS[:, 2, :], MREM[:, :], MPARTS[:, 1, :], ALU.subtract)
                    dve.drain().then_inc(mparts_ready, 1)
                for g, i in pieces:
                    qt, heads, _, n, _, slot = PIECES[i]
                    idx = g * NPC + i
                    dve.wait_ge(piece_full, b * G * NPC + idx + 1)
                    bank = 5 + RING["piece", g, i] % BANKS
                    src = PS[:, bank, 0:n * len(heads)].rearrange("p (m k) -> p m k", k=n)
                    nc.vector.tensor_reduce(MXP[:, slot, heads[0]:heads[0] + len(heads), qt], src,
                                            AX.X, ALU.max).then_inc(ring_read, 1)
                if finished is not None:
                    dve.drain()
                    nc.vector.tensor_tensor(NMAX[:, :].rearrange("p (j t) -> p j t", j=J), MXP[:, 0, :, :],
                                            MXP[:, 1, :, :], ALU.max)
                    dve.drain()
                    nc.vector.tensor_scalar(NMAX[:, :], NMAX[:, :], -1.0, None, ALU.mult)
                    dve.drain().then_inc(negmax_ready, 1)

            def attend(b, beside):
                for at in range(ATT):
                    maxima(b, *PLAN.get(("attend", at), NOTHING))
                    if finished_half(at - 2) is not None:
                        norm_outputs(b, finished_half(at - 2), 0.0, ("out", at) if ("out", at) in RING else None)
                    if beside:
                        if at in A_JOBS:
                            project(b + 1, A_JOBS.index(at))
                        if at == A_MAX0:
                            natural_relu(b + 1)
                        if at == A_PHI:
                            natural_phi()

            def soft_output(b, n):
                ms, rms, tmp = SM[:, 0, :], SM[:, 1, :], SM[:, 2, :]
                lg, eq, one, two = (LG[:, i, :, :] for i in range(4))
                top, second = SM[:, 8, :], SM[:, 9, :]

                def pick(values, best, hot):
                    nc.vector.tensor_reduce(best, values, AX.X, ALU.max)
                    dve.drain()
                    nc.vector.tensor_tensor(eq, values, wide(best, E), ALU.is_equal)
                    dve.drain()
                    nc.vector.tensor_tensor(eq, eq, rank, ALU.mult)
                    dve.drain()
                    nc.vector.tensor_reduce(SM[:, 10, :], eq, AX.X, ALU.max)
                    dve.drain()
                    nc.vector.tensor_tensor(hot, rank, wide(SM[:, 10, :], E), ALU.is_equal)
                    dve.drain()

                if n == L_TURN:
                    norm_outputs(b, 15, 0.0)
                if n == L_WO:
                    for m, bank in enumerate((3, 6)):
                        dve.wait_ge(swo_full, b * 2 + m + 1)
                        nc.vector.tensor_tensor(four(HROWS, m), rows_of(bank), four(X1, m), ALU.add)
                    dve.drain().then_inc(h_done, 1)
                if n == L_SUM:
                    dve.wait_ge(out_stored, 16 * (b + 1))
                    nc.vector.tensor_tensor(SUM[:, :, :], HROWS, X1[:, :, :], ALU.add)
                if n == L_RMS:
                    dve.wait_ge(squares_done, b + 1)
                    nc.vector.tensor_reduce(ms, NRM, AX.X, ALU.add)
                    dve.drain()
                    nc.vector.tensor_scalar(ms, ms, 1.0 / D, RMS_EPS, ALU.mult, ALU.add)
                    dve.drain()
                    seed(rms, ms)
                    newton(rms, ms, tmp)
                if n == L_RSB:
                    newton(rms, ms, tmp)
                    newton(rms, ms, tmp)
                if n == L_NRM:
                    nc.vector.tensor_tensor(NRM, HROWS, wide(rms, D), ALU.mult).then_inc(snormed, 1)
                if n == L_LOWER:
                    dve.wait_ge(upper_ready, b + 1)
                    nc.vector.tensor_tensor(XN[:, 1, :], XAT[:, :], XN[:, 0, :], ALU.subtract).then_inc(lower_ready, 1)
                if n == L_ROUTE:
                    dve.wait_ge(router_full, b + 1)
                    nc.vector.tensor_copy(lg, PS[:, 6, 0:NT * E].rearrange("p (t e) -> p t e", e=E))
                    dve.drain().then_inc(router_read, 1)
                    pick(lg, top, one)
                if n == L_ROUTE2:
                    nc.vector.scalar_tensor_tensor(LG[:, 4, :, :], one, LOWEST, lg, ALU.mult, ALU.add)
                    dve.drain()
                    pick(LG[:, 4, :, :], second, two)
                    nc.vector.tensor_tensor(SM[:, 4, :], second, top, ALU.subtract)
                    dve.drain().then_inc(gap_ready, 1)
                if n == L_WEIGHTS:
                    dve.wait_ge(gap_exp, b + 1)
                    nc.vector.tensor_scalar(SM[:, 11, :], SM[:, 5, :], 1.0, None, ALU.add)
                    dve.drain()
                    nc.vector.reciprocal(SM[:, 12, :], SM[:, 11, :])
                    dve.drain()
                    nc.vector.tensor_tensor(SM[:, 13, :], SM[:, 12, :], SM[:, 5, :], ALU.mult)
                    dve.drain()
                    nc.vector.tensor_tensor(one, one, wide(SM[:, 12, :], E), ALU.mult)
                    nc.vector.tensor_tensor(two, two, wide(SM[:, 13, :], E), ALU.mult)
                    dve.drain()
                    nc.vector.tensor_tensor(CW[:, :, :], one, two, ALU.add)
                    dve.drain()

            def split_weights(e):
                w, cols, stage = WG if e < E else WU, slice(e % E * HID, (e % E + 1) * HID), STAGE[:, e % 4, 0:HID]
                dve.wait_ge(staged[e % 4], 16 * (e // 4 + 1))
                nc.vector.tensor_copy(w[:, 0, cols], stage)
                dve.drain()
                nc.vector.tensor_tensor(w[:, 1, cols], stage, w[:, 0, cols], ALU.subtract)
                dve.drain().then_inc(weights_split, 1)

            def linear(b, soft):
                for n in range(CHUNKS):
                    if not soft and n in SPLIT_AT:
                        for e in range(SPLIT_AT.index(n) * 2, SPLIT_AT.index(n) * 2 + 2):
                            split_weights(e)
                    if n % 4 == 3 and n > 4:
                        norm_outputs(b, n // 4 - 1, LIN_EPS)
                    if soft:
                        soft_output(b - 1, n)

            def experts(b, beside):
                def last_norm(b, half, step):
                    tiles = range(4 * half, 4 * half + 4)
                    var, rstd, tmp = (SM[:, i, 4 * half:4 * half + 4] for i in (1, 2, 3))
                    if step == 0:
                        dve.wait_ge(expert_added, b * 2 * E + 2 * E + (half + 1) * E)
                        layer_stats(SUM, tiles)
                    if step == 1:
                        layer_variance(var, tiles)
                        seed(rstd, var)
                    if step == 2:
                        newton(rstd, var, tmp)
                        newton(rstd, var, tmp)
                    if step == 3:
                        newton(rstd, var, tmp)
                    if step == 4:
                        layer_apply(SUM, SUM, SM[:, 2, :], tiles)
                        if half == 1:
                            dve.drain().then_inc(out_ready, 1)

                for n in range(UNITS):
                    if beside:
                        maxima(b + 1, None, early_pieces(n), None)
                    dve.wait_ge(silu_done, b * UNITS + n + 1)
                    nc.vector.tensor_tensor(hidden[:, n // HT % 2, n % HT, :], WORK[:, 6 + n % 2, :],
                                            PS[:, 2 * (n % 2) + 1, :], ALU.mult).then_inc(hid_done, 1)
                    if not beside and n < 3:
                        soft_output(b, (L_ROUTE, L_ROUTE2, L_WEIGHTS)[n])
                    if E_FINAL <= n < E_FINAL + F_STEPS:
                        last_norm(b, 0, n - E_FINAL)
                    if beside:
                        prepare(b + 1, n, False)
                for step in range(F_STEPS):
                    last_norm(b, 1, step)

            for bank in (5, 4):
                nc.vector.memset(PS[:, bank, :], 0.0)
            dve.drain().then_inc(psum_cleared, 1)
            nc.vector.memset(VL[:, :, :, :], 1.0)
            nc.vector.memset(VS[:, :, :, :], 1.0)
            nc.vector.memset(MXP[:, :, :, :], LOWEST)
            dve.drain()
            dve.sem_inc(o_normed, 1)
            dve.sem_inc(parts_stored[0], 48)
            dve.sem_inc(parts_stored[1], 48)
            dve.sem_inc(y_read, 2 * E)
            dve.sem_inc(expert_added, 2 * E)
            dve.sem_inc(out_stored, 16)
            dve.wait_ge(weights_loaded, 16 * 2)
            for r in range(4):
                project(0, r)
            dve.wait_ge(consts_loaded, 16 * 4)
            for r in range(4, 8):
                project(0, r)
            natural_relu(0)
            natural_phi()
            for r in range(8, len(A_JOBS)):
                project(0, r)
            linear(0, False)
            dve.wait_ge(rope_loaded, 16)
            for n in range(UNITS):
                if n == E_V + 1:
                    for e in range(2 * len(SPLIT_AT), 2 * E):
                        split_weights(e)
                prepare(0, n, True)
            with dve.Fori(0, B - 1) as b:
                attend(b, True)
                linear(b + 1, True)
                experts(b, True)
            attend(B - 1, False)
            for n in (L_TURN, L_WO, L_SUM, L_RMS, L_RSB, L_NRM, L_LOWER):
                soft_output(B - 1, n)
            experts(B - 1, False)


def rope_tables():
    inv_freq = 1.0 / 10000.0 ** (np.arange(0, HD, 2, dtype=np.float32) / HD)
    freqs = np.einsum("i,j->ij", np.arange(T, dtype=np.float32), inv_freq)
    emb = np.concatenate([freqs, freqs], axis=-1)
    sign = np.where(np.arange(HD) < HD // 2, -1.0, 1.0).astype(np.float32)
    cos, sin = np.cos(emb), np.sin(emb) * sign
    return np.stack([np.tile(cos.T, (H, 1)), np.tile(sin.T, (H, 1))]).astype(np.float32)


def kernel(**inputs):
    import ml_dtypes
    import concourse.bacc as bacc
    from concourse.bass_utils import run_bass_kernel_spmd

    a = {k: np.asarray(v) for k, v in inputs.items()}
    turn = np.array([h * HD + (d + HD // 2) % HD for h in range(H) for d in range(HD)])
    x = a["L0_attn_x"].reshape(B * T, D)
    bf16 = ml_dtypes.bfloat16
    consts = np.concatenate([
        np.eye(P, dtype=np.float32),
        (np.arange(P)[:, None] // HD == np.arange(H)[None, :]).astype(np.float32),
        np.tile(np.arange(E, 0, -1, dtype=np.float32), (P, NT)),
    ], axis=1)
    causal = np.where(np.arange(P)[None, :] <= np.arange(P)[:, None], 0.0, -1e30)
    arrays = {
        "x_rows": x,
        "x_cols": x.T,
        "attn_w": np.concatenate([
            a["L0_attn_Wq"].T, a["L0_attn_Wk"].T, a["L0_attn_Wv"].T, a["L0_attn_Wo"].T,
            a["L0_ffn_wq"], a["L0_ffn_wq"][:, turn], a["L0_ffn_wk"], a["L0_ffn_wk"][:, turn],
            a["L0_ffn_wv"], a["L0_ffn_wo"]], axis=1),
        "cols": np.stack([a["L0_attn_bq"], a["L0_attn_bk"], a["L0_ffn_g1"], a["L0_ffn_g2"]], axis=1),
        "rows": np.tile(np.concatenate([a["L0_attn_bk"], a["L0_attn_bv"], a["L0_attn_bo"]]), (P, 1)),
        "consts": consts,
        "consts_b": np.stack([np.eye(P), causal]).astype(bf16),
        "stack_rows": np.stack([np.zeros((3, H // 2, T)), np.ones((3, H // 2, T))]).astype(bf16),
        "rope": rope_tables(),
        "w_router": a["L0_ffn_w_router"],
        "wg": a["L0_ffn_wg"],
        "wu": a["L0_ffn_wu"],
        "wd": a["L0_ffn_wd"],
    }
    arrays = {k: np.ascontiguousarray(v) for k, v in arrays.items()}
    nc = bacc.Bacc("TRN2", target_bir_lowering=False, num_devices=1)
    args = [nc.dram_tensor(f"in_{k}", v.shape, mybir.dt.from_np(v.dtype), kind="ExternalInput").ap()
            for k, v in arrays.items()]
    out = nc.dram_tensor("out", (B, T, D), F32, kind="ExternalOutput").ap()
    block_program(nc, *args, out)
    r = run_bass_kernel_spmd(nc, [{f"in_{k}": v for k, v in arrays.items()}], core_ids=[0])
    return r.results[0]["out"]
```
